# Optimizing a Trainium2 kernel written in Bass

```python
import numpy as np
import jax
import jax.numpy as jnp

def _softmax(x, axis=-1):
    return jax.nn.softmax(x, axis=axis)

def _gelu(x):
    return jax.nn.gelu(x, approximate=True)

def _silu(x):
    return jax.nn.silu(x)

def _sigmoid(x):
    return jax.nn.sigmoid(x)

def _layernorm(x, axis=-1, eps=1e-05):
    m = jnp.mean(x, axis=axis, keepdims=True)
    v = jnp.var(x, axis=axis, keepdims=True)
    return (x - m) / jnp.sqrt(v + eps)

def _scatter_add(tgt, idx, src, axis=0):
    return tgt.at[idx].add(src)

def _segment_sum(src, seg, n):
    return jax.ops.segment_sum(src, seg, n)
kernel_name = 'mk_adj_preln_d1_adj_r2_d8f14c'

def setup_inputs(seed: int=0):
    np.random.seed(seed)
    _w = jnp.asarray

    def _rec_inputs():
        import jax
        import jax.numpy as jnp
        _gk = jax.random.key(seed)
        x = -0.0005207 + 1.001 * jax.random.normal(jax.random.fold_in(_gk, 1), (4096, 128), jnp.float32)
        _a = jax.random.bernoulli(jax.random.fold_in(_gk, 2), 0.000488281, (4096, 4096))
        _a = jnp.logical_or(_a, jnp.swapaxes(_a, -1, -2))
        _a = jnp.logical_or(_a, jnp.eye(4096, dtype=bool))
        adj = _a.astype(jnp.int32)
        return (x, adj)
    x, adj = _rec_inputs()

    def _L0_gnn_setup():
        import jax, jax.numpy as jnp
        import numpy as np
        N = 4096
        D_IN = 128
        D_OUT = 128
        NEG_INF = -9000000000000000.0
        key = jax.random.key(seed)
        k1, k2, k3, k4 = jax.random.split(key, 4)
        node_features = jax.random.normal(k1, (N, D_IN), dtype=jnp.float32)
        adjacency_matrix = jax.random.randint(k2, (N, N), 0, 2, dtype=jnp.int32)
        W = jax.random.normal(k3, (D_OUT, D_IN), dtype=jnp.float32) / np.sqrt(D_IN)
        b_W = jnp.zeros((D_OUT,), dtype=jnp.float32)
        a_vec = jax.random.normal(k4, (2 * D_OUT,), dtype=jnp.float32) / np.sqrt(2 * D_OUT)
        b_a = jnp.zeros((1,), dtype=jnp.float32)
        return {'node_features': node_features, 'adjacency_matrix': adjacency_matrix, 'W': W, 'b_W': b_W, 'a_vec': a_vec, 'b_a': b_a}
    _L0_gnn_all = _L0_gnn_setup()
    _L0_gnn_in = {k: v for k, v in _L0_gnn_all.items() if k in ('W', 'b_W', 'a_vec', 'b_a')}
    del _L0_gnn_all
    return {'x': x, 'adj': adj, 'L0_gnn_W': _L0_gnn_in['W'], 'L0_gnn_b_W': _L0_gnn_in['b_W'], 'L0_gnn_a_vec': _L0_gnn_in['a_vec'], 'L0_gnn_b_a': _L0_gnn_in['b_a']}

def reference(x, adj, L0_gnn_W, L0_gnn_b_W, L0_gnn_a_vec, L0_gnn_b_a):
    import jax
    import jax.numpy as jnp

    def _L0_gnn_ref(node_features, adjacency_matrix, W, b_W, a_vec, b_a):
        import jax, jax.numpy as jnp
        import numpy as np
        N = 4096
        D_IN = 128
        D_OUT = 128
        NEG_INF = -9000000000000000.0
        h = node_features @ W.T + b_W
        a1, a2 = (a_vec[:D_OUT], a_vec[D_OUT:])
        e = (h @ a1)[:, None] + (h @ a2)[None, :] + b_a[0]
        e = jnp.where(e > 0, e, 0.2 * e)
        scores = jnp.where(adjacency_matrix > 0, e, jnp.float32(NEG_INF))
        attention = jax.nn.softmax(scores, axis=1)
        h_prime = attention @ h
        return h_prime
    h = jnp.maximum(_layernorm(x, axis=-1), 0.0)
    x = x + _L0_gnn_ref(h, adj, L0_gnn_W, L0_gnn_b_W, L0_gnn_a_vec, L0_gnn_b_a)
    return x

_drawn_inputs = setup_inputs


def setup_inputs(seed=0):
    import zlib

    import numpy as np

    out = dict(_drawn_inputs(seed))
    spreads = {'L0_gnn_b_W': (0.0, 0.1)}
    factors = {}
    for name, (base, spread) in spreads.items():
        noise = np.random.default_rng([zlib.crc32(name.encode()), seed]).standard_normal(out[name].shape)
        drawn = base * np.exp(spread * noise) if base else spread * noise
        out[name] = jnp.asarray(drawn.astype(out[name].dtype))
    for name, factor in factors.items():
        out[name] = (out[name] * factor).astype(out[name].dtype)
    return out
```

```python
from contextlib import ExitStack

import concourse.bass as bass
from concourse import mybir

P = 128
ALU = mybir.AluOpType
ACT = mybir.ActivationFunctionType
F32 = mybir.dt.float32
I32 = mybir.dt.int32
BF16 = mybir.dt.bfloat16
F16 = mybir.dt.float16
AX_X = mybir.AxisListType.X
AX_XY = mybir.AxisListType.XY
RMAX = bass.bass_isa.ReduceOp.max

LN_EPS = 1e-5
SLOPE = 0.2
NEG_INF = -9e15
FEATURE_TOP = 256.0
WEIGHT_TOP = 128.0
LOW_SCALE = 2048.0
SPREAD_MAX = 15.0


def gat_layer_kernel(nc, x, adj, W, b_W, a_vec, b_a, out):
    N, DIN = x.shape
    DOUT = W.shape[0]
    assert DIN == P and DOUT == P and N % P == 0
    NT = N // P
    NF = DOUT + 1
    BT = 8
    BC = BT * P
    NB = N // BC
    QC = N // 2
    PER = 2
    NIT = NT // PER
    LEAD = 2
    CT = 4
    NCH = NT // CT
    STEPS = 8

    with ExitStack() as ctx:
        def sb(name, shape, dt):
            return ctx.enter_context(nc.sbuf_tensor(name, shape, dt))

        def sem(name):
            return ctx.enter_context(nc.semaphore(name))

        adj_sb = sb("adj_sb", [P, 2 * PER, QC], I32)
        sgn = sb("sgn", [P, PER, N], BF16)
        code = sb("code", [P, PER, N], BF16)
        t_row = sb("t_row", [P, N], F32)
        ct = sb("ct", [P, 4, BC], F16)
        dt_ = sb("dt_", [P, 4, BC], F16)
        U = sb("U", [P, NT, 2 * NF], F16)
        V = sb("V", [P, NT, 2 * NF], F16)
        H = sb("H", [P, NT, NF], F32)
        x_sb = sb("x_sb", [P, NT, DIN], F32)
        Z = sb("Z", [P, NT, NF], F32)
        hT = sb("hT", [P, CT * P * 2], F32)
        fin = sb("fin", [P, PER, 2, 2 * NF], F32)
        mix = sb("mix", [P, PER, 3, DOUT], F32)
        Wn = sb("Wn", [P, DIN], F32)
        WT = sb("WT", [P, DOUT + 2], F32)
        a_sb = sb("a_sb", [P, 2], F32)
        b_col = sb("b_col", [P, 1], F32)
        b_row = sb("b_row", [P, DOUT], F32)
        ba_row = sb("ba_row", [P, 1], F32)
        ident = sb("ident", [P, P], F32)
        identb = sb("identb", [P, P], BF16)
        ones = sb("ones", [P, P], F32)
        wa2 = sb("wa2", [P, P], F32)
        bbc = sb("bbc", [P, P], F32)
        stats = sb("stats", [P, NT, 6], F32)
        mv = sb("mv", [P, NT, 2], F32)
        rstd = sb("rstd", [P, 2, NT], F32)
        cc = sb("cc", [P, 2], F32)
        scol = sb("scol", [P, NT], F32)
        negs = sb("negs", [P, NT], F32)
        tcol = sb("tcol", [P, NT], F32)
        zz = sb("zz", [P, 4, NT], F32)
        ab = sb("ab", [P, 2, NT], F32)
        ew = sb("ew", [P, 4, NT], F32)
        tmx = sb("tmx", [P, 2, NCH], F32)
        tt = sb("tt", [P, 8], F32)
        gg = sb("gg", [P, 8], F32)
        den = sb("den", [P, NT], F32)
        rg = sb("rg", [P, NT], F32)
        low_unit = sb("low_unit", [P, DOUT], F32)
        rden = sb("rden", [P, NT], F32)
        bad = sb("bad", [P, NT + 4], F32)
        flag = sb("flag", [P, 1], I32)
        c_half = sb("c_half", [P, 1], F32)
        c_one = sb("c_one", [P, 1], F32)
        c_eps = sb("c_eps", [P, 1], F32)
        vf = sb("vf", [P, 2, CT, NF], F32)
        vd = sb("vd", [P, 2, CT, NF], F32)

        ps_t = ctx.enter_context(nc.psum_tensor("ps_t", [P, 4, 512], F32))
        ps_a = ctx.enter_context(nc.psum_tensor("ps_a", [P, 4, 512], F32))

        def tbank(i):
            return ps_t[:, i, :].bitcast(BF16)

        s_adj = [sem(f"s_adj{i}") for i in range(2 * PER)]
        s_x = [sem(f"s_x{i}") for i in range(NCH // 2)]
        s_w = sem("s_w")
        s_cst = sem("s_cst")
        s_bbc = sem("s_bbc")
        s_wsq = sem("s_wsq")
        s_wT = sem("s_wT")
        s_wTs = sem("s_wTs")
        s_wa = sem("s_wa")
        s_was = sem("s_was")
        s_dve = sem("s_dve")
        s_act = sem("s_act")
        s_pl = sem("s_pl")
        s_g = sem("s_g")
        s_var = sem("s_var")
        s_std = sem("s_std")
        s_xn = sem("s_xn")
        s_xT = sem("s_xT")
        s_hT = sem("s_hT")
        s_h = sem("s_h")
        s_hs = sem("s_hs")
        s_tr = sem("s_tr")
        s_z = sem("s_z")
        s_T = sem("s_T")
        s_ew = sem("s_ew")
        s_vf = [sem("s_uf"), sem("s_vf")]
        s_hi = [sem("s_uhi"), sem("s_vhi")]
        s_df = [sem("s_udf"), sem("s_vdf")]
        s_lo = [sem("s_ulo"), sem("s_vlo")]
        sgn_ready = sem("sgn_ready")
        code_ready = sem("code_ready")
        tp_ready = sem("tp_ready")
        d_ready = sem("d_ready")
        c_ready = sem("c_ready")
        mm_done = sem("mm_done")
        fin_a = sem("fin_a")
        fin_b = sem("fin_b")
        s_den = sem("s_den")
        s_rden = sem("s_rden")
        s_rg = sem("s_rg")
        p_low = sem("p_low")
        p_sum = sem("p_sum")
        p_att = sem("p_att")
        res_ready = sem("res_ready")
        s_out = sem("s_out")
        s_bad = sem("s_bad")
        s_flag = sem("s_flag")
        g_adj = sem("g_adj")
        g_dve = sem("g_dve")
        g_sc = sem("g_sc")
        g_exp = sem("g_exp")
        g_tp = sem("g_tp")
        g_ev = sem("g_ev")
        g_mm = sem("g_mm")
        g_res = sem("g_res")
        g_out = sem("g_out")

        adj_t = adj.rearrange("(g p) n -> p g n", p=P)
        x_t = x.rearrange("(g p) d -> p g d", p=P)
        out_t = out.rearrange("(g p) d -> p g d", p=P)

        def chained(eng, s):
            count = [0]

            def step(ins):
                count[0] += 1
                ins.then_inc(s, 1)
                eng.wait_ge(s, count[0])
            return step

        with nc.Block() as block:
            @block.sync
            def _(sp):
                for c in range(0, NCH, 2):
                    sp.dma_start(x_sb[:, c * CT:(c + 2) * CT, :],
                                 x_t[:, c * CT:(c + 2) * CT, :]).then_inc(s_x[c // 2], 16)
                for h in range(2 * PER):
                    sp.dma_start(adj_sb[:, h, :],
                                 adj_t[:, h // 2, (h % 2) * QC:(h % 2 + 1) * QC]).then_inc(s_adj[h], 16)

            @block.gpsimd
            def _(pool):
                step = chained(pool, s_pl)
                nc.gpsimd.memset(ones[:], 1.0)
                step(nc.gpsimd.memset(ident[:], 0.0))
                step(nc.gpsimd.affine_select(out=ident[:], in_=ident[:], compare_op=ALU.not_equal, fill=1.0,
                                             base=0, pattern=[[-1, P]], channel_multiplier=1))
                nc.gpsimd.memset(c_half[:], -0.5)
                nc.gpsimd.memset(c_one[:], -1.0)
                nc.gpsimd.memset(low_unit[:], 1.0 / LOW_SCALE)
                nc.gpsimd.memset(c_eps[:], LN_EPS)
                nc.gpsimd.tensor_copy(identb[:], ident[:]).then_inc(s_cst, 1)
                pool.wait_ge(s_g, 1)
                nc.gpsimd.partition_all_reduce(gg[:, 3:4], gg[:, 2:3], P, RMAX).then_inc(s_g, 1)
                pool.wait_ge(s_ew, 2)
                for c in range(NCH):
                    r = slice(c * CT, (c + 1) * CT)
                    if c >= 1:
                        pool.wait_ge(s_lo[1], c)
                    nc.gpsimd.tensor_tensor(vf[:, 1], H[:, r, :],
                                            ew[:, 3, r].to_broadcast([P, CT, NF]), ALU.mult).then_inc(s_vf[1], 1)
                    pool.wait_ge(s_hi[1], c + 1)
                    nc.gpsimd.tensor_tensor(vd[:, 1], vf[:, 1], V[:, r, 0:NF], ALU.subtract).then_inc(s_df[1], 1)

            @block.scalar
            def _(act):
                act.dma_start(Wn[:], W).then_inc(s_w, 16)
                for k in range(2):
                    act.dma_start(a_sb[:, k:k + 1], a_vec[k * P:(k + 1) * P].rearrange("(p a) -> p a", a=1)
                                  ).then_inc(s_w, 16)
                act.dma_start(b_col[:], b_W.rearrange("(p a) -> p a", a=1)).then_inc(s_w, 16)
                act.dma_start(b_row[:], b_W.rearrange("(a n) -> a n", a=1).to_broadcast([P, 128])).then_inc(s_w, 16)
                act.dma_start(ba_row[:], b_a.rearrange("(a n) -> a n", a=1).to_broadcast([P, 1])).then_inc(s_w, 16)
                act.wait_ge(s_cst, 1)
                act.wait_ge(s_wsq, 1)
                nc.scalar.activation(gg[:, 1:2], gg[:, 0:1], ACT.Sqrt).then_inc(s_wsq, 1)
                act.wait_ge(s_var, 1)
                nc.scalar.activation(rstd[:, 0, :], mv[:, :, 1], ACT.Sqrt, bias=c_eps[:, 0:1]).then_inc(s_std, 1)
                for c in range(NCH):
                    act.wait_ge(s_xT, c + 1)
                    if c >= 2:
                        act.wait_ge(s_h, c - 1)
                    nc.scalar.activation(hT[:, (c % 2) * 512:(c % 2) * 512 + 512], ps_t[:, c % 2, :],
                                         ACT.Relu).then_inc(s_hT, 1)
                    act.wait_ge(s_h, c + 1)
                    act.wait_ge(s_was, 3)
                    nc.scalar.activation(t_row[:, c * 512:(c + 1) * 512], ps_t[:, 2 + c % 2, :],
                                         ACT.Identity, bias=cc[:, 1:2]).then_inc(s_tr, 1)
                act.wait_ge(s_z, 1)
                nc.scalar.activation(ew[:, 0, :], tcol[:], ACT.Exp, bias=tt[:, 2:3])
                nc.scalar.activation(ew[:, 1, :], tcol[:], ACT.Exp, bias=tt[:, 3:4], scale=SLOPE)
                nc.scalar.activation(ab[:, 0, :], zz[:, 1, :], ACT.Exp)
                nc.scalar.activation(ab[:, 1, :], zz[:, 2, :], ACT.Exp).then_inc(s_z, 1)
                for c in range(NCH):
                    r = slice(c * CT, (c + 1) * CT)
                    for k, dst in ((0, U), (1, V)):
                        act.wait_ge(s_vf[k], c + 1)
                        nc.scalar.activation(dst[:, r, 0:NF], vf[:, k], ACT.Copy).then_inc(s_hi[k], 1)
                    for k, dst in ((0, U), (1, V)):
                        act.wait_ge(s_df[k], c + 1)
                        nc.scalar.activation(dst[:, r, NF:2 * NF], vd[:, k], ACT.Copy,
                                             scale=LOW_SCALE).then_inc(s_lo[k], 1)

            @block.vector
            def _(dve):
                step = chained(dve, s_dve)
                dve.wait_ge(s_w, 96)
                step(nc.vector.tensor_tensor(bbc[:], Wn[:], Wn[:], ALU.mult))
                nc.vector.tensor_reduce(gg[:, 0:1], bbc[:], AX_X, ALU.add).then_inc(s_wsq, 1)
                dve.wait_ge(s_wsq, 2)
                step(nc.vector.scalar_tensor_tensor(gg[:, 4:5], b_col[:], -1.0, b_col[:], ALU.mult, ALU.max))
                step(nc.vector.tensor_scalar(gg[:, 5:6], gg[:, 1:2], 1.01 * float(DIN) ** 0.5, 1e-30,
                                             ALU.mult, ALU.max))
                nc.vector.tensor_tensor(gg[:, 2:3], gg[:, 5:6], gg[:, 4:5], ALU.add).then_inc(s_g, 1)
                dve.wait_ge(s_g, 2)
                step(nc.vector.reciprocal(gg[:, 6:7], gg[:, 3:4]))
                dve.wait_ge(s_cst, 1)
                nc.vector.tensor_scalar(H[:, :, DOUT], ones[:, 0:NT], gg[:, 3:4], None, ALU.mult)
                nc.vector.tensor_scalar(bbc[:], ones[:], b_col[:, 0:1], None, ALU.mult).then_inc(s_bbc, 1)
                dve.wait_ge(s_wT, 1)
                nc.vector.tensor_copy(WT[:, 0:DOUT], ps_a[:, 0, 0:DOUT]).then_inc(s_wTs, 1)
                dve.wait_ge(s_wa, 1)
                nc.vector.tensor_copy(WT[:, DOUT:DOUT + 2], ps_a[:, 1, 0:2]).then_inc(s_was, 1)
                nc.vector.tensor_scalar(wa2[:], ones[:], ps_a[:, 1, 1:2], None, ALU.mult).then_inc(s_was, 1)
                step(nc.vector.tensor_copy(cc[:], ps_a[:, 2, 0:2]))
                nc.vector.tensor_tensor(cc[:, 0:1], cc[:, 0:1], ba_row[:], ALU.add).then_inc(s_was, 1)
                for g in range(NT):
                    if g % (2 * CT) == 0:
                        dve.wait_ge(s_x[g // (2 * CT)], 16)
                    last = nc.vector.bn_stats(stats[:, g, :], x_sb[:, g, :])
                step(last)
                for g in range(NT):
                    last = nc.vector.bn_aggr(mv[:, g, :], stats[:, g, :])
                last.then_inc(s_var, 1)
                dve.wait_ge(s_std, 1)
                step(nc.vector.reciprocal(rstd[:, 1, :], rstd[:, 0, :]))

                def normalise(c):
                    for g in range(c * CT, (c + 1) * CT):
                        last = nc.vector.tensor_scalar(Z[:, g, 0:DIN], x_sb[:, g, :], mv[:, g, 0:1],
                                                       rstd[:, 1, g:g + 1], ALU.subtract, ALU.mult)
                    last.then_inc(s_xn, 1)

                normalise(0)
                normalise(1)
                for c in range(NCH):
                    if c + 2 < NCH:
                        normalise(c + 2)
                    k = 2 * (c % 2)
                    dve.wait_ge(s_h, c + 1)
                    for j in range(2):
                        nc.vector.tensor_tensor(
                            H[:, c * CT + 2 * j:c * CT + 2 * j + 2, 0:DOUT],
                            ps_a[:, k + j, 0:260].rearrange("p (a n) -> p a n", a=2)[:, :, 0:DOUT],
                            b_row[:].rearrange("p (a n) -> p a n", a=1).to_broadcast([P, 2, DOUT]), ALU.add)
                    for j in range(2):
                        r = slice(c * CT + 2 * j, c * CT + 2 * j + 2)
                        v = ps_a[:, k + j, 0:260].rearrange("p (a n) -> p a n", a=2)
                        nc.vector.tensor_scalar(scol[:, r], v[:, :, DOUT], cc[:, 0:1], None, ALU.add)
                        last = nc.vector.tensor_scalar(tcol[:, r], v[:, :, DOUT + 1], cc[:, 1:2], None, ALU.add)
                    last.then_inc(s_hs, 1)
                    dve.wait_ge(s_tr, c + 1)
                    nc.vector.tensor_reduce(tmx[:, 0, c:c + 1], t_row[:, c * 512:(c + 1) * 512], AX_X, ALU.max)
                    last = nc.vector.tensor_reduce(tmx[:, 1, c:c + 1], t_row[:, c * 512:(c + 1) * 512], AX_X, ALU.min)
                step(last)
                nc.vector.tensor_reduce(tt[:, 0:1], tmx[:, 0, :], AX_X, ALU.max)
                step(nc.vector.tensor_reduce(tt[:, 1:2], tmx[:, 1, :], AX_X, ALU.min))
                nc.vector.tensor_scalar(tt[:, 2:3], tt[:, 0:1], -1.0, None, ALU.mult)
                nc.vector.tensor_scalar(tt[:, 3:4], tt[:, 0:1], -SLOPE, None, ALU.mult)
                nc.vector.tensor_tensor(tt[:, 4:5], tt[:, 0:1], tt[:, 1:2], ALU.subtract)
                nc.vector.tensor_scalar(negs[:], scol[:], -1.0, None, ALU.mult)
                step(nc.vector.tensor_scalar(zz[:, 0, :], scol[:], tt[:, 0:1], 1.0 - SLOPE, ALU.add, ALU.mult))
                nc.vector.tensor_scalar(zz[:, 1, :], zz[:, 0, :], 0.0, None, ALU.min)
                nc.vector.tensor_scalar(bad[:, NT:NT + 1], tt[:, 4:5], SPREAD_MAX, -1.0, ALU.is_le, ALU.mult)
                nc.vector.tensor_scalar(zz[:, 2, :], zz[:, 0, :], -1.0, 0.0, ALU.mult, ALU.min).then_inc(s_z, 1)
                dve.wait_ge(s_z, 2)
                for k in range(2):
                    nc.vector.tensor_scalar(ew[:, 2 + k, :], ew[:, k, :], gg[:, 6:7], FEATURE_TOP * WEIGHT_TOP,
                                            ALU.mult, ALU.mult).then_inc(s_ew, 1)
                dve.wait_ge(s_ew, 2)
                for c in range(NCH):
                    r = slice(c * CT, (c + 1) * CT)
                    if c >= 1:
                        dve.wait_ge(s_lo[0], c)
                    nc.vector.tensor_tensor(vf[:, 0], H[:, r, :],
                                            ew[:, 2, r].to_broadcast([P, CT, NF]), ALU.mult).then_inc(s_vf[0], 1)
                    dve.wait_ge(s_hi[0], c + 1)
                    nc.vector.tensor_tensor(vd[:, 0], vf[:, 0], U[:, r, 0:NF], ALU.subtract).then_inc(s_df[0], 1)

            @block.tensor
            def _(pe):
                pe.wait_ge(s_cst, 1)
                pe.wait_ge(s_w, 96)
                nc.tensor.transpose(ps_a[:, 0, 0:P], Wn[:], ident[:]).then_inc(s_wT, 1)
                pe.wait_ge(s_bbc, 1)
                nc.tensor.matmul(ps_a[:, 1, 0:2], Wn[:], a_sb[:], start=True, stop=True)
                nc.tensor.matmul(ps_a[:, 2, 0:2], bbc[:], a_sb[:], start=True, stop=True).then_inc(s_wa, 1)
                pe.wait_ge(s_was, 3)
                pe.wait_ge(s_wTs, 1)

                def transposes(c):
                    pe.wait_ge(s_xn, c + 1)
                    if c >= 2:
                        pe.wait_ge(s_hT, c - 1)
                    for j in range(CT):
                        last = nc.tensor.transpose(ps_t[:, c % 2, j * P:(j + 1) * P],
                                                   Z[:, c * CT + j, 0:DIN], ident[:])
                    last.then_inc(s_xT, 1)

                transposes(0)
                for c in range(NCH):
                    if c + 1 < NCH:
                        transposes(c + 1)
                    pe.wait_ge(s_hT, c + 1)
                    if c >= 2:
                        pe.wait_ge(s_hs, c - 1)
                        pe.wait_ge(s_tr, c - 1)
                    h = hT[:, (c % 2) * 512:(c % 2) * 512 + 512]
                    for j in range(CT):
                        nc.tensor.matmul(ps_a[:, 2 * (c % 2) + j // 2, (j % 2) * 130:(j % 2) * 130 + 130],
                                         h[:, j * P:(j + 1) * P], WT[:], start=(j % 2 == 0), stop=(j % 2 == 1),
                                         skip_group_check=True)
                    nc.tensor.matmul(ps_t[:, 2 + c % 2, :], wa2[:], h, start=True, stop=True).then_inc(s_h, 1)

        with nc.Block() as block:
            def rounds(eng, body):
                body(0)
                with eng.Fori(1, NIT - 1) as it:
                    body(it)
                body(NIT - 1)

            def past(eng, s, it, per, value):
                if isinstance(it, int):
                    if per * it + value > 0:
                        eng.wait_ge(s, per * it + value)
                else:
                    eng.wait_ge(s, it * per + value)

            def last_round(it):
                return isinstance(it, int) and it == NIT - 1

            def finish_step(k, stage):
                return NB * (k + 1) + LEAD + 1 + stage

            def finishes(it, n, stages, finish):
                for k in range(PER):
                    for stage in range(stages):
                        back, at = divmod(finish_step(k, stage), PER * NB)
                        if at == n and not (isinstance(it, int) and it < back):
                            finish(it - back, k, stage)

            def finishes_after(stages, finish):
                for k in range(PER):
                    for stage in range(stages):
                        if finish_step(k, stage) >= PER * NB:
                            finish(NIT - 1, k, stage)

            @block.sync
            def _(sp):
                def load(it):
                    tile = [sp.snap(it * PER + k) if not isinstance(it, int) else it * PER + k for k in range(PER)]
                    for h in range(2 * PER):
                        past(sp, sgn_ready, it, 2 * PER, h + 1 - 2 * PER)
                        sp.dma_start(adj_sb[:, h:h + 1, :],
                                     adj_t[:, bass.ds(tile[h // 2], 1), (h % 2) * QC:(h % 2 + 1) * QC]
                                     ).then_inc(s_adj[h], 16)

                def store(it):
                    first = it * PER if isinstance(it, int) else sp.snap(it * PER)
                    past(sp, res_ready, it, PER, PER)
                    sp.dma_start(out_t[:, bass.ds(first, PER), :],
                                 Z[:, bass.ds(first, PER), 0:DOUT]).then_inc(s_out, 16)

                load(1)
                with sp.Fori(2, NIT) as it:
                    load(it)
                    store(it - 2)
                store(NIT - 2)
                store(NIT - 1)
                sp.wait_ge(s_out, 16 * NIT)

            @block.scalar
            def _(act):
                def signs(it, h):
                    past(act, s_adj[h], it, 16, 16)
                    past(act, code_ready, it, PER * NB, 2 * h + 2 - PER * NB)
                    nc.scalar.activation(sgn[:, h // 2, (h % 2) * QC:(h % 2 + 1) * QC], adj_sb[:, h, :], ACT.Sign,
                                         bias=c_half[:, 0:1]).then_inc(sgn_ready, 1)

                def c_part(it, n):
                    past(act, d_ready, it, PER * NB, n + 1)
                    past(act, mm_done, it, PER * NB, n + 1 - 4)
                    nc.scalar.activation(ct[:, n % 4, :], tbank(n % 4), ACT.Relu,
                                         bias=c_one[:, 0:1]).then_inc(c_ready, 1)

                def finish(it, k, stage):
                    past(act, mm_done, it, PER * NB, NB * (k + 1))
                    past(act, res_ready, it, PER, k + 1 - PER)
                    nc.scalar.activation(fin[:, k, 0, :], ps_a[:, 2 * k, 0:2 * NF], ACT.Copy,
                                         scale=ab[:, 0, bass.ds(it * PER + k, 1)]).then_inc(fin_a, 1)

                def body(it):
                    for n in range(PER * NB):
                        if n % 2 == 0:
                            h = n // 2 + 2
                            if h < 2 * PER:
                                signs(it, h)
                            elif not last_round(it):
                                signs(it + 1, h - 2 * PER)
                        c_part(it, n)
                        finishes(it, n, 1, finish)

                signs(0, 0)
                signs(0, 1)
                rounds(act, body)
                finishes_after(1, finish)

            @block.vector
            def _(dve):
                def codes(it, n):
                    past(dve, sgn_ready, it, 2 * PER, n // 2 + 1)
                    past(dve, tp_ready, it, PER * NB, n + 1 - PER * NB)
                    r = slice((n % NB) * BC, (n % NB + 1) * BC)
                    nc.vector.scalar_tensor_tensor(code[:, n // NB, r], t_row[:, r],
                                                   negs[:, bass.ds(it * PER + n // NB, 1)],
                                                   sgn[:, n // NB, r], ALU.is_gt, ALU.add).then_inc(code_ready, 1)

                def d_part(it, n):
                    past(dve, tp_ready, it, PER * NB, n + 1)
                    past(dve, mm_done, it, PER * NB, n + 1 - 4)
                    nc.vector.tensor_scalar(dt_[:, n % 4, :], tbank(n % 4), 1.0, None,
                                            ALU.is_equal).then_inc(d_ready, 1)

                def finish(it, k, stage):
                    g = bass.ds(it * PER + k, 1)
                    if stage == 0:
                        past(dve, fin_a, it, PER, k + 1)
                        nc.vector.scalar_tensor_tensor(fin[:, k, 1, :], ps_a[:, 2 * k + 1, 0:2 * NF],
                                                       ab[:, 1, g], fin[:, k, 0, :],
                                                       ALU.mult, ALU.add).then_inc(fin_b, 1)
                    elif stage == 1:
                        past(dve, fin_b, it, PER, k + 1)
                        nc.vector.scalar_tensor_tensor(den[:, g], fin[:, k, 1, 2 * NF - 1:2 * NF], 1.0 / LOW_SCALE,
                                                       fin[:, k, 1, DOUT:NF], ALU.mult, ALU.add).then_inc(s_den, 1)
                    elif stage == 2:
                        past(dve, s_den, it, PER, k + 1)
                        nc.vector.reciprocal(rden[:, g], den[:, g]).then_inc(s_rden, 1)
                    else:
                        past(dve, s_rden, it, PER, k + 1)
                        nc.vector.tensor_scalar(rg[:, g], rden[:, g], gg[:, 3:4], None,
                                                ALU.mult).then_inc(s_rg, 1)

                def body(it):
                    for n in range(PER * NB):
                        if n + LEAD < PER * NB:
                            codes(it, n + LEAD)
                        elif not last_round(it):
                            codes(it + 1, n + LEAD - PER * NB)
                        d_part(it, n)
                        finishes(it, n, 4, finish)

                for n in range(LEAD):
                    codes(0, n)
                rounds(dve, body)
                finishes_after(4, finish)
                dve.wait_ge(s_den, NT)
                nc.vector.tensor_scalar(bad[:, 0:NT], den[:], 0.0, -1.0, ALU.is_gt, ALU.mult).then_inc(s_bad, 1)
                dve.wait_ge(s_bad, 1)
                nc.vector.tensor_reduce(bad[:, NT + 1:NT + 2], bad[:, 0:NT + 1], AX_X, ALU.max).then_inc(s_bad, 1)
                dve.wait_ge(s_bad, 3)
                nc.vector.tensor_scalar(flag[:], bad[:, NT + 2:NT + 3], 1.0, None, ALU.add).then_inc(s_flag, 1)

            @block.gpsimd
            def _(pool):
                with pool.Fori(0, NIT) as it:
                    for k in range(PER):
                        g = bass.ds(it * PER + k, 1)
                        pool.wait_ge(fin_b, it * PER + k + 1)
                        nc.gpsimd.tensor_tensor(mix[:, k, 0, :], fin[:, k, 1, NF:2 * NF - 1], low_unit[:],
                                                ALU.mult).then_inc(p_low, 1)
                        pool.wait_ge(p_low, it * PER + k + 1)
                        nc.gpsimd.tensor_tensor(mix[:, k, 1, :], mix[:, k, 0, :],
                                                fin[:, k, 1, 0:DOUT], ALU.add).then_inc(p_sum, 1)
                        pool.wait_ge(p_sum, it * PER + k + 1)
                        pool.wait_ge(s_rg, it * PER + k + 1)
                        nc.gpsimd.tensor_tensor(mix[:, k, 2, :], mix[:, k, 1, :],
                                                rg[:, g].to_broadcast([P, DOUT]), ALU.mult).then_inc(p_att, 1)
                        pool.wait_ge(p_att, it * PER + k + 1)
                        nc.gpsimd.tensor_tensor(Z[:, g, 0:DOUT], mix[:, k, 2:3, :], x_sb[:, g, :],
                                                ALU.add).then_inc(res_ready, 1)
                pool.wait_ge(s_bad, 2)
                nc.gpsimd.partition_all_reduce(bad[:, NT + 2:NT + 3], bad[:, NT + 1:NT + 2], P,
                                               RMAX).then_inc(s_bad, 1)

            @block.tensor
            def _(pe):
                def transposes(it, n):
                    past(pe, code_ready, it, PER * NB, n + 1)
                    past(pe, c_ready, it, PER * NB, n + 1 - 4)
                    for j in range(BT):
                        col = (n % NB) * BC + j * P
                        ins = nc.tensor.transpose(tbank(n % 4)[:, j * P:(j + 1) * P],
                                                  code[:, n // NB, col:col + P], identb[:])
                    ins.then_inc(tp_ready, 1)

                def products(it, n):
                    k = n // NB
                    past(pe, c_ready, it, PER * NB, n + 1)
                    if n % NB == 0:
                        past(pe, fin_b, it, PER, k + 1 - PER)
                    for j in range(BT):
                        jt = (n % NB) * BT + j
                        for m, (part, data) in enumerate(((ct, U), (dt_, V))):
                            ins = nc.tensor.matmul(ps_a[:, 2 * k + m, 0:2 * NF], part[:, n % 4, j * P:(j + 1) * P],
                                                   data[:, jt, :], start=(jt == 0), stop=(jt == NT - 1))
                    ins.then_inc(mm_done, 1)

                def body(it):
                    for n in range(PER * NB):
                        if n + LEAD < PER * NB:
                            transposes(it, n + LEAD)
                        elif not last_round(it):
                            transposes(it + 1, n + LEAD - PER * NB)
                        products(it, n)

                for n in range(LEAD):
                    transposes(0, n)
                rounds(pe, body)

        with nc.Block() as block:
            halves = [adj_sb[:, 0:2, :].rearrange("p a n -> p (a n)"),
                      adj_sb[:, 2:4, :].rearrange("p a n -> p (a n)").bitcast(F32),
                      sgn[:, :, :].rearrange("p a n -> p (a n)").bitcast(F32)]
            conn, score, keep = halves
            pT = hT
            acc = ps_a[:, 0, 0:NF]

            def needed(eng):
                return eng.value_load(flag[0:1, 0:1], min_val=0, max_val=1)

            @block.gpsimd
            def _(pool):
                with pool.If(needed(pool) > 0):
                    with pool.Fori(0, NT) as g:
                        pool.dma_start(conn, adj_t[:, bass.ds(g, 1), :]).then_inc(g_adj, 16)
                        pool.wait_ge(g_res, g + 1)
                        pool.dma_start(out_t[:, bass.ds(g, 1), :], Z[:, bass.ds(g, 1), 0:DOUT]).then_inc(g_out, 16)
                        pool.wait_ge(g_out, g * 16 + 16)

            @block.vector
            def _(dve):
                with dve.If(needed(dve) > 0):
                    with dve.Fori(0, NT) as g:
                        g1 = bass.ds(g, 1)
                        done = [0]

                        def step(ins):
                            done[0] += 1
                            ins.then_inc(g_dve, 1)
                            dve.wait_ge(g_dve, g * STEPS + done[0])

                        dve.wait_ge(g_adj, g * 16 + 16)
                        step(nc.vector.tensor_scalar(score, t_row[:], scol[:, g1], None, ALU.add))
                        step(nc.vector.scalar_tensor_tensor(score, score, SLOPE, score, ALU.mult, ALU.max))
                        step(nc.vector.tensor_scalar(keep, conn, 0.0, None, ALU.is_gt))
                        step(nc.vector.tensor_tensor(score, score, keep, ALU.mult))
                        step(nc.vector.tensor_scalar(keep, keep, -1.0, -NEG_INF, ALU.add, ALU.mult))
                        step(nc.vector.tensor_tensor(score, score, keep, ALU.add))
                        step(nc.vector.tensor_reduce(tt[:, 5:6], score, AX_X, ALU.max))
                        nc.vector.tensor_scalar(tt[:, 6:7], tt[:, 5:6], -1.0, None, ALU.mult).then_inc(g_sc, 1)
                        dve.wait_ge(g_mm, g * (NT // 4) + NT // 4)
                        step(nc.vector.reciprocal(rden[:, g1], den[:, g1]))
                        nc.vector.scalar_tensor_tensor(Z[:, g1, 0:DOUT], ps_a[:, 0:1, 0:DOUT], rden[:, g1],
                                                       x_sb[:, g1, :], ALU.mult, ALU.add).then_inc(g_res, 1)
                        assert done[0] == STEPS

            @block.scalar
            def _(act):
                with act.If(needed(act) > 0):
                    with act.Fori(0, NT) as g:
                        act.wait_ge(g_sc, g + 1)
                        nc.scalar.activation(keep, score, ACT.Exp, bias=tt[:, 6:7],
                                             accum_out=den[:, bass.ds(g, 1)]).then_inc(g_exp, 1)
                        for q in range(NT // 4):
                            act.wait_ge(g_tp, g * (NT // 4) + q + 1)
                            nc.scalar.activation(pT[:, 0:512], ps_t[:, 0, :], ACT.Copy).then_inc(g_ev, 1)
                            act.wait_ge(g_mm, g * (NT // 4) + q + 1)

            @block.tensor
            def _(pe):
                with pe.If(needed(pe) > 0):
                    with pe.Fori(0, NT) as g:
                        pe.wait_ge(g_exp, g + 1)
                        for q in range(NT // 4):
                            for j in range(4):
                                ins = nc.tensor.transpose(ps_t[:, 0, j * P:(j + 1) * P],
                                                          keep[:, (4 * q + j) * P:(4 * q + j + 1) * P], ident[:])
                            ins.then_inc(g_tp, 1)
                            pe.wait_ge(g_ev, g * (NT // 4) + q + 1)
                            for j in range(4):
                                jt = 4 * q + j
                                ins = nc.tensor.matmul(acc[:, 0:DOUT], pT[:, j * P:(j + 1) * P], H[:, jt, 0:DOUT],
                                                       start=(jt == 0), stop=(jt == NT - 1))
                            ins.then_inc(g_mm, 1)
                        pe.wait_ge(g_res, g + 1)


_INS = ["x", "adj", "L0_gnn_W", "L0_gnn_b_W", "L0_gnn_a_vec", "L0_gnn_b_a"]


def kernel(**inputs):
    import numpy as np
    import concourse.bacc as bacc
    from concourse.bass_utils import run_bass_kernel_spmd

    nc = bacc.Bacc("TRN2", target_bir_lowering=False, num_devices=1)
    arrays, args = {}, []
    for name in _INS:
        a = np.ascontiguousarray(inputs[name])
        arrays[f"in_{name}"] = a
        args.append(nc.dram_tensor(f"in_{name}", a.shape, mybir.dt.from_np(a.dtype), kind="ExternalInput").ap())
    out = nc.dram_tensor("out", arrays["in_x"].shape, mybir.dt.float32, kind="ExternalOutput").ap()
    gat_layer_kernel(nc, *args, out)
    r = run_bass_kernel_spmd(nc, [arrays], core_ids=[0])
    return r.results[0]["out"]
```

```python
import math
from contextlib import ExitStack

import concourse.bass as bass
from concourse import mybir

P = 128
ALU = mybir.AluOpType
ACT = mybir.ActivationFunctionType
F32 = mybir.dt.float32
I32 = mybir.dt.int32
BF16 = mybir.dt.bfloat16
F16 = mybir.dt.float16
AX_X = mybir.AxisListType.X
AX_XY = mybir.AxisListType.XY
RMAX = bass.bass_isa.ReduceOp.max

LN_EPS = 1e-5
SLOPE = 0.2
NEG_INF = -9e15
LOW_SCALE = 2048.0
SHIFT = 11 * math.log(2.0)
SHIFT_MAX = 2.75
SPREAD_MAX = 12.0


def gat_layer_kernel(nc, x, adj, W, b_W, a_vec, b_a, out):
    N, DIN = x.shape
    DOUT = W.shape[0]
    assert DIN == P and DOUT == P and N % P == 0
    NT = N // P
    NF = DOUT + 1
    BT = 8
    BC = BT * P
    NB = N // BC
    QC = N // 2
    PER = 2
    NIT = NT // PER
    LEAD = 2
    AHEAD = 3
    CT = 4
    NCH = NT // CT
    STEPS = 8

    with ExitStack() as ctx:
        def sb(name, shape, dt):
            return ctx.enter_context(nc.sbuf_tensor(name, shape, dt))

        def sem(name):
            return ctx.enter_context(nc.semaphore(name))

        adj_sb = sb("adj_sb", [P, 2 * PER, QC], I32)
        sgn = sb("sgn", [P, PER, N], BF16)
        code = sb("code", [P, PER, N], BF16)
        t_row = sb("t_row", [P, N], F32)
        ct = sb("ct", [P, 4, BC], F16)
        dt_ = sb("dt_", [P, 4, BC], F16)
        U = sb("U", [P, NT, 2 * NF], F16)
        V = sb("V", [P, NT, 2 * NF], F16)
        H = sb("H", [P, NT, NF], F32)
        x_sb = sb("x_sb", [P, NT, DIN], F32)
        Z = sb("Z", [P, NT, NF], F32)
        hT = sb("hT", [P, CT * P * 2], F32)
        fin = sb("fin", [P, PER, 2, 2 * NF], F32)
        mix = sb("mix", [P, PER, 3, DOUT], F32)
        Wn = sb("Wn", [P, DIN], F32)
        WT = sb("WT", [P, DOUT + 2], F32)
        a_sb = sb("a_sb", [P, 2], F32)
        b_col = sb("b_col", [P, 1], F32)
        b_row = sb("b_row", [P, DOUT], F32)
        ba_row = sb("ba_row", [P, 1], F32)
        ident = sb("ident", [P, P], F32)
        identb = sb("identb", [P, P], BF16)
        ones = sb("ones", [P, P], F32)
        wa2 = sb("wa2", [P, P], F32)
        bbc = sb("bbc", [P, P], F32)
        stats = sb("stats", [P, NT, 6], F32)
        mv = sb("mv", [P, NT, 2], F32)
        rstd = sb("rstd", [P, 2, NT], F32)
        cc = sb("cc", [P, 2], F32)
        scol = sb("scol", [P, NT], F32)
        negs = sb("negs", [P, NT], F32)
        tcol = sb("tcol", [P, NT], F32)
        zz = sb("zz", [P, 4, NT], F32)
        ab = sb("ab", [P, 2, NT], F32)
        ew = sb("ew", [P, 4, NT], F32)
        tmx = sb("tmx", [P, 2, NCH], F32)
        tt = sb("tt", [P, 10], F32)
        gg = sb("gg", [P, 8], F32)
        den = sb("den", [P, NT], F32)
        rg = sb("rg", [P, NT], F32)
        low_unit = sb("low_unit", [P, DOUT], F32)
        rden = sb("rden", [P, NT], F32)
        bad = sb("bad", [P, NT + 4], F32)
        flag = sb("flag", [P, 1], I32)
        c_half = sb("c_half", [P, 1], F32)
        c_one = sb("c_one", [P, 1], F32)
        c_eps = sb("c_eps", [P, 1], F32)
        uf = sb("uf", [P, 2, CT, NF], F32)
        wsq = uf[:, 0, 0, 0:DIN]
        vf = sb("vf", [P, 2, CT, NF], F32)
        vd = sb("vd", [P, 2, CT, NF], F32)
        tx = sb("tx", [P, 3], F32)
        warm = sb("warm", [P, 1], F32)

        ps_t = ctx.enter_context(nc.psum_tensor("ps_t", [P, 4, 512], F32))
        ps_a = ctx.enter_context(nc.psum_tensor("ps_a", [P, 4, 512], F32))

        def tbank(i):
            return ps_t[:, i, :].bitcast(BF16)

        s_adj = [sem(f"s_adj{i}") for i in range(2 * PER)]
        s_x = [sem(f"s_x{i}") for i in range(NCH // 2)]
        s_w = sem("s_w")
        s_cst = sem("s_cst")
        s_bbc = sem("s_bbc")
        s_wsq = sem("s_wsq")
        s_wT = sem("s_wT")
        s_wTs = sem("s_wTs")
        s_wa = sem("s_wa")
        s_was = sem("s_was")
        s_dve = sem("s_dve")
        s_act = sem("s_act")
        s_pl = sem("s_pl")
        s_g = sem("s_g")
        s_var = sem("s_var")
        s_std = sem("s_std")
        s_xn = sem("s_xn")
        s_xT = sem("s_xT")
        s_hT = sem("s_hT")
        s_h = sem("s_h")
        s_hs = sem("s_hs")
        s_tr = sem("s_tr")
        s_z = sem("s_z")
        s_ew = sem("s_ew")
        u_low = sem("u_low")
        v_scaled = sem("v_scaled")
        v_high = sem("v_high")
        v_left = sem("v_left")
        v_low = sem("v_low")
        s_b = sem("s_b")
        s_R = sem("s_R")
        s_s = sem("s_s")
        s_gate = sem("s_gate")
        s_st = sem("s_st")
        s_hd = sem("s_hd")
        s_tp = sem("s_tp")
        s_neg = sem("s_neg")
        s_ab = sem("s_ab")
        s_idb = sem("s_idb")
        s_xb = sem("s_xb")
        sgn_ready = sem("sgn_ready")
        code_ready = sem("code_ready")
        tp_ready = sem("tp_ready")
        d_ready = sem("d_ready")
        c_ready = sem("c_ready")
        mm_done = sem("mm_done")
        fin_a = sem("fin_a")
        fin_b = sem("fin_b")
        s_den = sem("s_den")
        s_rden = sem("s_rden")
        s_rg = sem("s_rg")
        p_low = sem("p_low")
        p_sum = sem("p_sum")
        p_att = sem("p_att")
        res_ready = sem("res_ready")
        s_out = sem("s_out")
        s_bad = sem("s_bad")
        s_flag = sem("s_flag")
        g_adj = sem("g_adj")
        g_dve = sem("g_dve")
        g_sc = sem("g_sc")
        g_exp = sem("g_exp")
        g_tp = sem("g_tp")
        g_ev = sem("g_ev")
        g_mm = sem("g_mm")
        g_res = sem("g_res")
        g_out = sem("g_out")

        adj_t = adj.rearrange("(g p) n -> p g n", p=P)
        x_t = x.rearrange("(g p) d -> p g d", p=P)
        out_t = out.rearrange("(g p) d -> p g d", p=P)

        def chained(eng, s):
            count = [0]

            def step(ins):
                count[0] += 1
                ins.then_inc(s, 1)
                eng.wait_ge(s, count[0])
            return step

        with nc.Block() as block:
            def rounds(eng, body, first=1):
                for it in range(first):
                    body(it)
                with eng.Fori(first, NIT - 1) as it:
                    body(it)
                body(NIT - 1)

            def past(eng, s, it, per, value):
                if isinstance(it, int):
                    if per * it + value > 0:
                        eng.wait_ge(s, per * it + value)
                else:
                    eng.wait_ge(s, it * per + value)

            def last_round(it):
                return isinstance(it, int) and it == NIT - 1

            def hooked(step, before):
                def body(it):
                    for n in range(PER * NB):
                        if isinstance(it, int) and it == 0 and n in before:
                            before[n]()
                        step(it, n)
                return body

            def finish_step(k, stage):
                return NB * (k + 1) + LEAD + stage

            def finishes(it, n, stages, finish):
                for k in range(PER):
                    for stage in stages:
                        back, at = divmod(finish_step(k, stage), PER * NB)
                        if at == n and not (isinstance(it, int) and it < back):
                            finish(it - back, k, stage)

            def finishes_after(stages, finish):
                for k in range(PER):
                    for stage in stages:
                        if finish_step(k, stage) >= PER * NB:
                            finish(NIT - 1, k, stage)

            @block.sync
            def _(sp):
                def load_x(c):
                    r = slice(2 * c * CT, 2 * (c + 1) * CT)
                    sp.dma_start(x_sb[:, r, :], x_t[:, r, :]).then_inc(s_x[c], 16)

                load_x(0)
                sp.dma_start(Wn[:], W).then_inc(s_w, 16)
                for k in range(2):
                    sp.dma_start(a_sb[:, k:k + 1], a_vec[k * P:(k + 1) * P].rearrange("(p a) -> p a", a=1)
                                 ).then_inc(s_w, 16)
                sp.dma_start(b_col[:], b_W.rearrange("(p a) -> p a", a=1)).then_inc(s_w, 16)
                for c in range(1, NCH // 2):
                    load_x(c)
                sp.dma_start(ba_row[:], b_a.rearrange("(a n) -> a n", a=1).to_broadcast([P, 1])).then_inc(s_b, 16)
                sp.dma_start(b_row[:], b_W.rearrange("(a n) -> a n", a=1).to_broadcast([P, DOUT])).then_inc(s_b, 16)
                for h in range(2 * PER):
                    sp.dma_start(adj_sb[:, h, :],
                                 adj_t[:, h // 2, (h % 2) * QC:(h % 2 + 1) * QC]).then_inc(s_adj[h], 16)

                def load(it):
                    tile = [sp.snap(it * PER + k) if not isinstance(it, int) else it * PER + k for k in range(PER)]
                    for h in range(2 * PER):
                        past(sp, sgn_ready, it, 2 * PER, h + 1 - 2 * PER)
                        sp.dma_start(adj_sb[:, h:h + 1, :],
                                     adj_t[:, bass.ds(tile[h // 2], 1), (h % 2) * QC:(h % 2 + 1) * QC]
                                     ).then_inc(s_adj[h], 16)

                def store(it):
                    first = it * PER if isinstance(it, int) else sp.snap(it * PER)
                    past(sp, res_ready, it, PER, PER)
                    sp.dma_start(out_t[:, bass.ds(first, PER), :],
                                 Z[:, bass.ds(first, PER), 0:DOUT]).then_inc(s_out, 16)

                load(1)
                with sp.Fori(2, NIT) as it:
                    load(it)
                    store(it - 2)
                store(NIT - 2)
                store(NIT - 1)
                sp.wait_ge(s_out, 16 * NIT)

            @block.scalar
            def _(act):
                def signs(it, h):
                    past(act, s_adj[h], it, 16, 16)
                    past(act, code_ready, it, PER * NB, 2 * h + 2 - PER * NB)
                    nc.scalar.activation(sgn[:, h // 2, (h % 2) * QC:(h % 2 + 1) * QC], adj_sb[:, h, :], ACT.Sign,
                                         bias=c_half[:, 0:1]).then_inc(sgn_ready, 1)

                def c_part(it, n):
                    past(act, d_ready, it, PER * NB, n + 1)
                    past(act, mm_done, it, PER * NB, n + 1 - 4)
                    nc.scalar.activation(ct[:, n % 4, :], tbank(n % 4), ACT.Relu,
                                         bias=c_one[:, 0:1]).then_inc(c_ready, 1)

                def finish(it, k, stage):
                    past(act, mm_done, it, PER * NB, NB * (k + 1))
                    past(act, res_ready, it, PER, k + 1 - PER)
                    nc.scalar.activation(fin[:, k, 0, :], ps_a[:, 2 * k, 0:2 * NF], ACT.Copy,
                                         scale=ab[:, 0, bass.ds(it * PER + k, 1)]).then_inc(fin_a, 1)

                def relu_chunk(c):
                    act.wait_ge(s_xT, c + 1)
                    if c >= 2:
                        act.wait_ge(s_h, c - 1)
                    nc.scalar.activation(hT[:, (c % 2) * 512:(c % 2) * 512 + 512], ps_t[:, c % 2, :],
                                         ACT.Relu).then_inc(s_hT, 1)

                def take_chunk(c):
                    act.wait_ge(s_h, c + 1)
                    nc.scalar.activation(t_row[:, c * 512:(c + 1) * 512], ps_t[:, 2 + c % 2, :],
                                         ACT.Identity, bias=cc[:, 1:2]).then_inc(s_tr, 1)
                    act.wait_ge(s_st, c + 1)
                    k = 2 * (c % 2)
                    nc.scalar.activation(
                        H[:, c * CT:(c + 1) * CT, 0:DOUT].rearrange("p (k a) n -> p k a n", k=2),
                        ps_a[:, k:k + 2, 0:2 * (DOUT + 2)].rearrange("p k (a n) -> p k a n", a=2)[:, :, :, 0:DOUT],
                        ACT.Copy).then_inc(s_hs, 1)

                def high(c):
                    act.wait_ge(v_scaled, c + 1)
                    nc.scalar.activation(V[:, c * CT:(c + 1) * CT, 0:NF], vf[:, c % 2], ACT.Copy).then_inc(v_high, 1)

                def low(c):
                    act.wait_ge(v_left, c + 1)
                    nc.scalar.activation(V[:, c * CT:(c + 1) * CT, NF:2 * NF], vd[:, c % 2], ACT.Copy,
                                         scale=LOW_SCALE).then_inc(v_low, 1)

                act.wait_ge(s_cst, 1)
                act.wait_ge(s_wsq, 1)
                nc.scalar.activation(gg[:, 1:2], gg[:, 0:1], ACT.Sqrt).then_inc(s_wsq, 1)
                act.wait_ge(s_var, NCH // 2)
                nc.scalar.activation(rstd[:, 0, :], mv[:, :, 1], ACT.Sqrt, bias=c_eps[:, 0:1]).then_inc(s_std, 1)
                nc.scalar.activation(warm[:], c_half[:], ACT.Exp)

                def weights(q):
                    r = slice(2 * CT * q, 2 * CT * (q + 1))
                    if q == 0:
                        act.wait_ge(s_R, 1)
                    act.wait_ge(s_st, 2 * q + 2)
                    nc.scalar.activation(ew[:, 0, r], tcol[:, r], ACT.Exp, bias=tt[:, 2:3]).then_inc(s_ew, 1)
                    nc.scalar.activation(ew[:, 1, r], tcol[:, r], ACT.Exp, bias=tt[:, 3:4],
                                         scale=SLOPE).then_inc(s_ew, 1)

                def row_factors():
                    act.wait_ge(s_z, 2)
                    nc.scalar.activation(ab[:, 0, :], zz[:, 1, :], ACT.Exp)
                    nc.scalar.activation(ab[:, 1, :], zz[:, 3, :], ACT.Exp).then_inc(s_ab, 1)

                relu_chunk(0)
                act.wait_ge(s_was, 3)
                for c in range(NCH):
                    if c + 1 < NCH:
                        relu_chunk(c + 1)
                    take_chunk(c)
                    if c % 2 == 1:
                        weights(c // 2)
                    elif c >= 2:
                        signs(0, c // 2 - 1)
                    if 2 <= c < NCH - 1:
                        high(c - 2)
                    if 3 <= c < NCH - 1:
                        low(c - 3)
                signs(0, 3)

                def split_v(*pieces):
                    for kind, c in pieces:
                        kind(c)

                before = {
                    0: lambda: split_v((high, 5), (low, 4)),
                    1: lambda: split_v((high, 6), (low, 5)),
                    2: lambda: split_v((high, 7), (low, 6), (low, 7)),
                    3: row_factors,
                }

                def step(it, n):
                    if n % 2 == 0 and not (isinstance(it, int) and it == 0 and n == 0):
                        h = n // 2 + AHEAD
                        if h < 2 * PER:
                            signs(it, h)
                        elif not last_round(it):
                            signs(it + 1, h - 2 * PER)
                    c_part(it, n)
                    finishes(it, n, [0], finish)

                rounds(act, hooked(step, before), first=2)
                finishes_after([0], finish)

            @block.vector
            def _(dve):
                step_ = chained(dve, s_dve)

                def codes(it, n):
                    past(dve, sgn_ready, it, 2 * PER, n // 2 + 1)
                    past(dve, tp_ready, it, PER * NB, n + 1 - PER * NB)
                    r = slice((n % NB) * BC, (n % NB + 1) * BC)
                    nc.vector.scalar_tensor_tensor(code[:, n // NB, r], t_row[:, r],
                                                   negs[:, bass.ds(it * PER + n // NB, 1)],
                                                   sgn[:, n // NB, r], ALU.is_gt, ALU.add).then_inc(code_ready, 1)

                def d_part(it, n):
                    past(dve, tp_ready, it, PER * NB, n + 1)
                    past(dve, mm_done, it, PER * NB, n + 1 - 4)
                    nc.vector.tensor_scalar(dt_[:, n % 4, :], tbank(n % 4), 1.0, None,
                                            ALU.is_equal).then_inc(d_ready, 1)

                def finish(it, k, stage):
                    g = bass.ds(it * PER + k, 1)
                    if stage == 1:
                        past(dve, fin_a, it, PER, k + 1)
                        nc.vector.scalar_tensor_tensor(fin[:, k, 1, :], ps_a[:, 2 * k + 1, 0:2 * NF],
                                                       ab[:, 1, g], fin[:, k, 0, :],
                                                       ALU.mult, ALU.add).then_inc(fin_b, 1)
                    elif stage == 2:
                        past(dve, fin_b, it, PER, k + 1)
                        nc.vector.scalar_tensor_tensor(den[:, g], fin[:, k, 1, 2 * NF - 1:2 * NF], 1.0 / LOW_SCALE,
                                                       fin[:, k, 1, DOUT:NF], ALU.mult, ALU.add).then_inc(s_den, 1)
                    elif stage == 3:
                        past(dve, s_den, it, PER, k + 1)
                        nc.vector.reciprocal(rden[:, g], den[:, g]).then_inc(s_rden, 1)
                    else:
                        past(dve, s_rden, it, PER, k + 1)
                        nc.vector.tensor_scalar(rg[:, g], rden[:, g], gg[:, 3:4], None,
                                                ALU.mult).then_inc(s_rg, 1)

                def statistics(q):
                    dve.wait_ge(s_x[q], 16)
                    for g in range(2 * CT * q, 2 * CT * (q + 1)):
                        last = nc.vector.bn_stats(stats[:, g, :], x_sb[:, g, :])
                    step_(last)
                    for g in range(2 * CT * q, 2 * CT * (q + 1)):
                        last = nc.vector.bn_aggr(mv[:, g, :], stats[:, g, :])
                    last.then_inc(s_var, 1)

                def normalise(c):
                    for g in range(c * CT, (c + 1) * CT):
                        last = nc.vector.tensor_scalar(Z[:, g, 0:DIN], x_sb[:, g, :], mv[:, g, 0:1],
                                                       rstd[:, 1, g:g + 1], ALU.subtract, ALU.mult)
                    last.then_inc(s_xn, 1)

                def s_and_t(c):
                    k = 2 * (c % 2)
                    r = slice(c * CT, (c + 1) * CT)
                    v = ps_a[:, k:k + 2, 0:2 * (DOUT + 2)].rearrange("p k (a n) -> p k a n", a=2)
                    dve.wait_ge(s_h, c + 1)
                    nc.vector.tensor_scalar(scol[:, r].rearrange("p (k a) -> p k a", k=2), v[:, :, :, DOUT],
                                            cc[:, 0:1], None, ALU.add).then_inc(s_s, 1)
                    nc.vector.tensor_scalar(tcol[:, r].rearrange("p (k a) -> p k a", k=2), v[:, :, :, DOUT + 1],
                                            cc[:, 1:2], None, ALU.add).then_inc(s_st, 1)
                    dve.wait_ge(s_s, c + 1)
                    nc.vector.tensor_scalar(negs[:, r], scol[:, r], -1.0, None, ALU.mult).then_inc(s_neg, 1)

                def split_u(c):
                    r = slice(c * CT, (c + 1) * CT)
                    dve.wait_ge(s_ew, 2 * (c // 2) + 2)
                    dve.wait_ge(s_hs, c + 1)
                    step_(nc.vector.tensor_tensor(uf[:, 0], H[:, r, :],
                                                  ew[:, 0, r].to_broadcast([P, CT, NF]), ALU.mult))
                    step_(nc.vector.tensor_copy(U[:, r, 0:NF], uf[:, 0]))
                    if c >= 1:
                        dve.wait_ge(u_low, c)
                    step_(nc.vector.tensor_tensor(uf[:, 1], uf[:, 0], U[:, r, 0:NF], ALU.subtract))
                    nc.vector.tensor_scalar(U[:, r, NF:2 * NF], uf[:, 1], LOW_SCALE, None, ALU.mult).then_inc(u_low, 1)

                statistics(0)
                dve.wait_ge(s_w, 64)
                step_(nc.vector.tensor_tensor(wsq, Wn[:], Wn[:], ALU.mult))
                nc.vector.tensor_reduce(gg[:, 0:1], wsq, AX_X, ALU.add).then_inc(s_wsq, 1)
                dve.wait_ge(s_cst, 1)
                nc.vector.tensor_scalar(bbc[:], ones[:], b_col[:, 0:1], None, ALU.mult).then_inc(s_bbc, 1)
                nc.vector.tensor_scalar(H[:, :, DOUT], ones[:, 0:NT], 1.0, None, ALU.mult).then_inc(s_hd, 1)
                statistics(1)
                dve.wait_ge(s_wsq, 2)
                nc.vector.tensor_scalar(gg[:, 2:3], gg[:, 1:2], 1.01 * float(DIN) ** 0.5, 1e-30,
                                        ALU.mult, ALU.max).then_inc(s_g, 1)
                statistics(2)
                statistics(3)
                dve.wait_ge(s_std, 1)
                step_(nc.vector.reciprocal(rstd[:, 1, :], rstd[:, 0, :]))
                normalise(0)
                dve.wait_ge(s_g, 2)
                step_(nc.vector.reciprocal(gg[:, 6:7], gg[:, 3:4]))
                dve.wait_ge(s_wT, 1)
                nc.vector.tensor_scalar(WT[:, 0:DOUT], ps_a[:, 0, 0:DOUT], gg[:, 6:7], None, ALU.mult).then_inc(s_wTs, 1)
                dve.wait_ge(s_wa, 1)
                nc.vector.tensor_copy(WT[:, DOUT:DOUT + 2], ps_a[:, 1, 0:2]).then_inc(s_was, 1)
                nc.vector.tensor_scalar(wa2[:], ones[:], ps_a[:, 1, 1:2], None, ALU.mult).then_inc(s_was, 1)
                step_(nc.vector.tensor_copy(cc[:], ps_a[:, 2, 0:2]))
                dve.wait_ge(s_b, 32)
                nc.vector.tensor_tensor(cc[:, 0:1], cc[:, 0:1], ba_row[:], ALU.add).then_inc(s_was, 1)
                dve.wait_ge(s_was, 3)
                normalise(1)
                normalise(2)

                def scale_point():
                    dve.wait_ge(s_tp, 2)
                    nc.vector.tensor_scalar(tt[:, 2:3], tx[:, 0:1], -1.0, SHIFT, ALU.mult, ALU.add)
                    nc.vector.tensor_scalar(tt[:, 3:4], tx[:, 0:1], -SLOPE, SHIFT, ALU.mult, ALU.add).then_inc(s_R, 1)

                for c in range(NCH):
                    if c + 3 < NCH:
                        normalise(c + 3)
                    s_and_t(c)
                    if c == 0:
                        dve.wait_ge(s_st, 1)
                        nc.vector.tensor_reduce(tt[:, 0:1], tcol[:, 0:CT], AX_X, ALU.max).then_inc(s_tp, 1)
                    if c == 1:
                        scale_point()
                    if c in (3, 5, 7):
                        split_u(c - 3)
                        split_u(c - 2)
                    if c in (4, 6):
                        dve.wait_ge(s_neg, 1)
                        dve.wait_ge(s_tr, c - 2)
                        codes(0, c // 2 - 2)
                dve.wait_ge(s_st, NCH)
                nc.vector.tensor_reduce(tt[:, 4:5], tcol[:], AX_X, ALU.max)
                nc.vector.tensor_reduce(tt[:, 5:6], tcol[:], AX_X, ALU.min, negate=True).then_inc(s_tp, 1)
                dve.wait_ge(s_neg, NCH)
                dve.wait_ge(s_tr, NCH)

                def row_exponents():
                    dve.wait_ge(s_tp, 4)
                    step_(nc.vector.tensor_tensor(tt[:, 6:7], tx[:, 1:2], tx[:, 0:1], ALU.subtract))
                    nc.vector.tensor_scalar(tt[:, 7:8], tt[:, 6:7], SLOPE, None, ALU.mult)
                    nc.vector.tensor_tensor(tt[:, 8:9], tx[:, 1:2], tx[:, 2:3], ALU.add)
                    nc.vector.tensor_scalar(zz[:, 0, :], scol[:], tx[:, 1:2], 1.0 - SLOPE, ALU.add, ALU.mult)
                    step_(nc.vector.tensor_scalar(zz[:, 2, :], scol[:], tx[:, 1:2], SLOPE - 1.0, ALU.add, ALU.mult))
                    nc.vector.tensor_scalar(zz[:, 1, :], zz[:, 0, :], 0.0, tt[:, 6:7], ALU.min,
                                            ALU.subtract).then_inc(s_z, 1)
                    nc.vector.tensor_scalar(zz[:, 3, :], zz[:, 2, :], 0.0, tt[:, 7:8], ALU.min,
                                            ALU.subtract).then_inc(s_z, 1)
                    nc.vector.tensor_scalar(bad[:, NT:NT + 1], tt[:, 8:9], SPREAD_MAX, -1.0, ALU.is_le, ALU.mult)
                    nc.vector.tensor_scalar(bad[:, NT + 1:NT + 2], tt[:, 6:7], SHIFT_MAX, -1.0, ALU.is_le,
                                            ALU.mult).then_inc(s_gate, 1)

                def step(it, n):
                    if n + LEAD < PER * NB:
                        codes(it, n + LEAD)
                    elif not last_round(it):
                        codes(it + 1, n + LEAD - PER * NB)
                    d_part(it, n)
                    finishes(it, n, [1, 2, 3, 4], finish)

                before = {1: lambda: split_u(6), 2: lambda: (split_u(7), row_exponents())}
                rounds(dve, hooked(step, before))
                finishes_after([1, 2, 3, 4], finish)
                dve.wait_ge(s_den, NT)
                dve.wait_ge(s_gate, 1)
                nc.vector.tensor_scalar(bad[:, 0:NT], den[:], 0.0, -1.0, ALU.is_gt, ALU.mult).then_inc(s_bad, 1)
                dve.wait_ge(s_bad, 1)
                nc.vector.tensor_reduce(bad[:, NT + 2:NT + 3], bad[:, 0:NT + 2], AX_X, ALU.max).then_inc(s_bad, 1)
                dve.wait_ge(s_bad, 3)
                nc.vector.tensor_scalar(flag[:], bad[:, NT + 3:NT + 4], 1.0, None, ALU.add).then_inc(s_flag, 1)

            @block.gpsimd
            def _(pool):
                step = chained(pool, s_pl)
                nc.gpsimd.memset(ones[:], 1.0)
                nc.gpsimd.memset(c_half[:], -0.5)
                nc.gpsimd.memset(c_one[:], -1.0)
                nc.gpsimd.memset(c_eps[:], LN_EPS)
                step(nc.gpsimd.memset(ident[:], 0.0))
                nc.gpsimd.affine_select(out=ident[:], in_=ident[:], compare_op=ALU.not_equal, fill=1.0,
                                        base=0, pattern=[[-1, P]], channel_multiplier=1).then_inc(s_cst, 1)
                pool.wait_ge(s_cst, 1)
                nc.gpsimd.tensor_copy(identb[:], ident[:]).then_inc(s_idb, 1)
                nc.gpsimd.memset(low_unit[:], 1.0 / LOW_SCALE).then_inc(s_idb, 1)

                pool.wait_ge(s_g, 1)
                nc.gpsimd.partition_all_reduce(gg[:, 3:4], gg[:, 2:3], P, RMAX).then_inc(s_g, 1)
                pool.wait_ge(s_tp, 1)
                nc.gpsimd.partition_all_reduce(tx[:, 0:1], tt[:, 0:1], P, RMAX).then_inc(s_tp, 1)

                def scale_v(c):
                    r = slice(c * CT, (c + 1) * CT)
                    pool.wait_ge(s_ew, 2 * (c // 2) + 2)
                    pool.wait_ge(s_hs, c + 1)
                    if c >= 2:
                        pool.wait_ge(v_left, c - 1)
                    nc.gpsimd.tensor_tensor(vf[:, c % 2], H[:, r, :],
                                            ew[:, 1, r].to_broadcast([P, CT, NF]), ALU.mult).then_inc(v_scaled, 1)

                def left_v(c):
                    pool.wait_ge(v_high, c + 1)
                    if c >= 2:
                        pool.wait_ge(v_low, c - 1)
                    nc.gpsimd.tensor_tensor(vd[:, c % 2], vf[:, c % 2], V[:, c * CT:(c + 1) * CT, 0:NF],
                                            ALU.subtract).then_inc(v_left, 1)

                pool.wait_ge(s_hd, 1)
                scale_v(0)
                for c in range(NCH):
                    if c + 1 < NCH:
                        scale_v(c + 1)
                    left_v(c)
                pool.wait_ge(s_tp, 3)
                nc.gpsimd.partition_all_reduce(tx[:, 1:3], tt[:, 4:6], P, RMAX).then_inc(s_tp, 1)
                pool.wait_ge(s_xn, NCH)
                pool.wait_ge(s_b, 32)
                for q in range(NCH // 2):
                    r = slice(2 * CT * q, 2 * CT * (q + 1))
                    nc.gpsimd.tensor_tensor(x_sb[:, r, :], x_sb[:, r, :],
                                            b_row[:].rearrange("p (a n) -> p a n", a=1).to_broadcast([P, 2 * CT, DIN]),
                                            ALU.add).then_inc(s_xb, 1)
                pool.wait_ge(s_idb, 2)
                pool.wait_ge(s_xb, NCH // 2)
                with pool.Fori(0, NIT) as it:
                    for k in range(PER):
                        g = bass.ds(it * PER + k, 1)
                        pool.wait_ge(fin_b, it * PER + k + 1)
                        nc.gpsimd.tensor_tensor(mix[:, k, 0, :], fin[:, k, 1, NF:2 * NF - 1], low_unit[:],
                                                ALU.mult).then_inc(p_low, 1)
                        pool.wait_ge(p_low, it * PER + k + 1)
                        nc.gpsimd.tensor_tensor(mix[:, k, 1, :], mix[:, k, 0, :],
                                                fin[:, k, 1, 0:DOUT], ALU.add).then_inc(p_sum, 1)
                        pool.wait_ge(p_sum, it * PER + k + 1)
                        pool.wait_ge(s_rg, it * PER + k + 1)
                        nc.gpsimd.tensor_tensor(mix[:, k, 2, :], mix[:, k, 1, :],
                                                rg[:, g].to_broadcast([P, DOUT]), ALU.mult).then_inc(p_att, 1)
                        pool.wait_ge(p_att, it * PER + k + 1)
                        nc.gpsimd.tensor_tensor(Z[:, g, 0:DOUT], mix[:, k, 2:3, :], x_sb[:, g, :],
                                                ALU.add).then_inc(res_ready, 1)
                pool.wait_ge(s_bad, 2)
                nc.gpsimd.partition_all_reduce(bad[:, NT + 3:NT + 4], bad[:, NT + 2:NT + 3], P,
                                               RMAX).then_inc(s_bad, 1)

            @block.tensor
            def _(pe):
                def transposes(it, n):
                    past(pe, code_ready, it, PER * NB, n + 1)
                    past(pe, c_ready, it, PER * NB, n + 1 - 4)
                    for j in range(BT):
                        col = (n % NB) * BC + j * P
                        ins = nc.tensor.transpose(tbank(n % 4)[:, j * P:(j + 1) * P],
                                                  code[:, n // NB, col:col + P], identb[:])
                    ins.then_inc(tp_ready, 1)

                def products(it, n):
                    k = n // NB
                    past(pe, c_ready, it, PER * NB, n + 1)
                    if isinstance(it, int) and it == 0 and n < NB:
                        pe.wait_ge(u_low, 2 * n + 2)
                        pe.wait_ge(v_low, 2 * n + 2)
                    if n % NB == 0:
                        past(pe, fin_b, it, PER, k + 1 - PER)
                    for j in range(BT):
                        jt = (n % NB) * BT + j
                        for m, (part, data) in enumerate(((ct, U), (dt_, V))):
                            ins = nc.tensor.matmul(ps_a[:, 2 * k + m, 0:2 * NF], part[:, n % 4, j * P:(j + 1) * P],
                                                   data[:, jt, :], start=(jt == 0), stop=(jt == NT - 1))
                    ins.then_inc(mm_done, 1)

                pe.wait_ge(s_cst, 1)
                pe.wait_ge(s_w, 64)
                nc.tensor.transpose(ps_a[:, 0, 0:P], Wn[:], ident[:]).then_inc(s_wT, 1)
                pe.wait_ge(s_bbc, 1)
                nc.tensor.matmul(ps_a[:, 1, 0:2], Wn[:], a_sb[:], start=True, stop=True)
                nc.tensor.matmul(ps_a[:, 2, 0:2], bbc[:], a_sb[:], start=True, stop=True).then_inc(s_wa, 1)

                def turn_chunk(c):
                    pe.wait_ge(s_xn, c + 1)
                    if c >= 2:
                        pe.wait_ge(s_hT, c - 1)
                    for j in range(CT):
                        last = nc.tensor.transpose(ps_t[:, c % 2, j * P:(j + 1) * P],
                                                   Z[:, c * CT + j, 0:DIN], ident[:])
                    last.then_inc(s_xT, 1)

                turn_chunk(0)
                pe.wait_ge(s_was, 3)
                pe.wait_ge(s_wTs, 1)
                for c in range(NCH):
                    if c + 1 < NCH:
                        turn_chunk(c + 1)
                    pe.wait_ge(s_hT, c + 1)
                    if c >= 2:
                        pe.wait_ge(s_hs, c - 1)
                        pe.wait_ge(s_tr, c - 1)
                    h = hT[:, (c % 2) * 512:(c % 2) * 512 + 512]
                    for j in range(CT):
                        at = (j % 2) * (DOUT + 2)
                        nc.tensor.matmul(ps_a[:, 2 * (c % 2) + j // 2, at:at + DOUT + 2],
                                         h[:, j * P:(j + 1) * P], WT[:], start=(j % 2 == 0), stop=(j % 2 == 1),
                                         skip_group_check=True)
                    nc.tensor.matmul(ps_t[:, 2 + c % 2, :], wa2[:], h, start=True, stop=True).then_inc(s_h, 1)
                pe.wait_ge(s_idb, 2)
                pe.wait_ge(s_tr, NCH)
                pe.wait_ge(s_hs, NCH)

                def step(it, n):
                    if n + LEAD < PER * NB:
                        transposes(it, n + LEAD)
                    elif not last_round(it):
                        transposes(it + 1, n + LEAD - PER * NB)
                    products(it, n)

                for n in range(LEAD):
                    transposes(0, n)
                rounds(pe, hooked(step, {}))

        with nc.Block() as block:
            halves = [adj_sb[:, 0:2, :].rearrange("p a n -> p (a n)"),
                      adj_sb[:, 2:4, :].rearrange("p a n -> p (a n)").bitcast(F32),
                      sgn[:, :, :].rearrange("p a n -> p (a n)").bitcast(F32)]
            conn, score, keep = halves
            pT = hT
            acc = ps_a[:, 0, 0:NF]

            def needed(eng):
                return eng.value_load(flag[0:1, 0:1], min_val=0, max_val=1)

            @block.gpsimd
            def _(pool):
                with pool.If(needed(pool) > 0):
                    with pool.Fori(0, NT) as g:
                        pool.dma_start(conn, adj_t[:, bass.ds(g, 1), :]).then_inc(g_adj, 16)
                        pool.wait_ge(g_res, g + 1)
                        pool.dma_start(out_t[:, bass.ds(g, 1), :], Z[:, bass.ds(g, 1), 0:DOUT]).then_inc(g_out, 16)
                        pool.wait_ge(g_out, g * 16 + 16)

            @block.vector
            def _(dve):
                with dve.If(needed(dve) > 0):
                    with dve.Fori(0, NT) as g:
                        g1 = bass.ds(g, 1)
                        done = [0]

                        def step(ins):
                            done[0] += 1
                            ins.then_inc(g_dve, 1)
                            dve.wait_ge(g_dve, g * STEPS + done[0])

                        dve.wait_ge(g_adj, g * 16 + 16)
                        step(nc.vector.tensor_scalar(score, t_row[:], scol[:, g1], None, ALU.add))
                        step(nc.vector.scalar_tensor_tensor(score, score, SLOPE, score, ALU.mult, ALU.max))
                        step(nc.vector.tensor_scalar(keep, conn, 0.0, None, ALU.is_gt))
                        step(nc.vector.tensor_tensor(score, score, keep, ALU.mult))
                        step(nc.vector.tensor_scalar(keep, keep, -1.0, -NEG_INF, ALU.add, ALU.mult))
                        step(nc.vector.tensor_tensor(score, score, keep, ALU.add))
                        nc.vector.tensor_reduce(tt[:, 9:10], score, AX_X, ALU.max, negate=True).then_inc(g_sc, 1)
                        dve.wait_ge(g_mm, g * (NT // 4) + NT // 4)
                        step(nc.vector.reciprocal(rden[:, g1], den[:, g1]))
                        step(nc.vector.tensor_scalar(rg[:, g1], rden[:, g1], gg[:, 3:4], None, ALU.mult))
                        nc.vector.scalar_tensor_tensor(Z[:, g1, 0:DOUT], ps_a[:, 0:1, 0:DOUT], rg[:, g1],
                                                       x_sb[:, g1, :], ALU.mult, ALU.add).then_inc(g_res, 1)
                        assert done[0] == STEPS

            @block.scalar
            def _(act):
                with act.If(needed(act) > 0):
                    with act.Fori(0, NT) as g:
                        act.wait_ge(g_sc, g + 1)
                        nc.scalar.activation(keep, score, ACT.Exp, bias=tt[:, 9:10],
                                             accum_out=den[:, bass.ds(g, 1)]).then_inc(g_exp, 1)
                        for q in range(NT // 4):
                            act.wait_ge(g_tp, g * (NT // 4) + q + 1)
                            nc.scalar.activation(pT[:, 0:512], ps_t[:, 0, :], ACT.Copy).then_inc(g_ev, 1)
                            act.wait_ge(g_mm, g * (NT // 4) + q + 1)

            @block.tensor
            def _(pe):
                with pe.If(needed(pe) > 0):
                    with pe.Fori(0, NT) as g:
                        pe.wait_ge(g_exp, g + 1)
                        for q in range(NT // 4):
                            for j in range(4):
                                ins = nc.tensor.transpose(ps_t[:, 0, j * P:(j + 1) * P],
                                                          keep[:, (4 * q + j) * P:(4 * q + j + 1) * P], ident[:])
                            ins.then_inc(g_tp, 1)
                            pe.wait_ge(g_ev, g * (NT // 4) + q + 1)
                            for j in range(4):
                                jt = 4 * q + j
                                ins = nc.tensor.matmul(acc[:, 0:DOUT], pT[:, j * P:(j + 1) * P], H[:, jt, 0:DOUT],
                                                       start=(jt == 0), stop=(jt == NT - 1))
                            ins.then_inc(g_mm, 1)
                        pe.wait_ge(g_res, g + 1)


_INS = ["x", "adj", "L0_gnn_W", "L0_gnn_b_W", "L0_gnn_a_vec", "L0_gnn_b_a"]


def kernel(**inputs):
    import numpy as np
    import concourse.bacc as bacc
    from concourse.bass_utils import run_bass_kernel_spmd

    nc = bacc.Bacc("TRN2", target_bir_lowering=False, num_devices=1)
    arrays, args = {}, []
    for name in _INS:
        a = np.ascontiguousarray(inputs[name])
        arrays[f"in_{name}"] = a
        args.append(nc.dram_tensor(f"in_{name}", a.shape, mybir.dt.from_np(a.dtype), kind="ExternalInput").ap())
    out = nc.dram_tensor("out", arrays["in_x"].shape, mybir.dt.float32, kind="ExternalOutput").ap()
    gat_layer_kernel(nc, *args, out)
    r = run_bass_kernel_spmd(nc, [arrays], core_ids=[0])
    return r.results[0]["out"]
```

```python
import math
from contextlib import ExitStack

import concourse.bass as bass
from concourse import mybir

P = 128
ALU = mybir.AluOpType
ACT = mybir.ActivationFunctionType
F32 = mybir.dt.float32
I32 = mybir.dt.int32
BF16 = mybir.dt.bfloat16
F16 = mybir.dt.float16
AX_X = mybir.AxisListType.X
RMAX = bass.bass_isa.ReduceOp.max

LN_EPS = 1e-5
SLOPE = 0.2
NEG_INF = -9e15
SHIFT = 13 * math.log(2.0)
SHIFT_MAX = 1.9
SPREAD_MAX = 8.0


def gat_layer_kernel(nc, x, adj, W, b_W, a_vec, b_a, out):
    N, DIN = x.shape
    DOUT = W.shape[0]
    assert DIN == P and DOUT == P and N % P == 0
    NT = N // P
    NF = DOUT + 1
    BT = 8
    BC = BT * P
    NB = N // BC
    QC = N // 2
    PER = 2
    NIT = NT // PER
    LEAD = 2
    CODES = 2
    BEHIND = 2
    AHEAD = 3
    CT = 4
    NCH = NT // CT
    BY_DVE, BY_POOL = (0, 2, 6), (1, 3, 4, 5, 7)
    STEPS = 8

    with ExitStack() as ctx:
        def sb(name, shape, dt):
            return ctx.enter_context(nc.sbuf_tensor(name, shape, dt))

        def sem(name):
            return ctx.enter_context(nc.semaphore(name))

        adj_sb = sb("adj_sb", [P, 2 * PER, QC], I32)
        sgn = sb("sgn", [P, PER, N], BF16)
        code = sb("code", [P, PER, N], BF16)
        t_row = sb("t_row", [P, N], F32)
        cT = sb("cT", [P, 4, BC], F16)
        dT = sb("dT", [P, 4, BC], F16)
        U = sb("U", [P, NT, 2 * NF], F16)
        V = sb("V", [P, NT, 2 * NF], F16)
        H = sb("H", [P, NT, NF], F32)
        x_sb = sb("x_sb", [P, NT, DIN], F32)
        Z = sb("Z", [P, NT, NF], F32)
        hT = sb("hT", [P, 2 * CT * P], F32)
        fin = sb("fin", [P, PER, 2, 2 * NF], F32)
        mix = sb("mix", [P, PER, 2, DOUT], F32)
        Wn = sb("Wn", [P, DIN], F32)
        WT = sb("WT", [P, DOUT + 2], F32)
        a_sb = sb("a_sb", [P, 2], F32)
        b_col = sb("b_col", [P, 1], F32)
        b_row = sb("b_row", [P, DOUT], F32)
        ba_row = sb("ba_row", [P, 1], F32)
        ident = sb("ident", [P, P], F32)
        identb = sb("identb", [P, P], BF16)
        ones = sb("ones", [P, P], F32)
        wa2 = sb("wa2", [P, P], F32)
        b_mat = sb("b_mat", [P, P], F32)
        stats = sb("stats", [P, NT, 6], F32)
        mv = sb("mv", [P, NT, 2], F32)
        rstd = sb("rstd", [P, 2, NT], F32)
        cc = sb("cc", [P, 2], F32)
        scol = sb("scol", [P, NT], F32)
        negs = sb("negs", [P, NT], F32)
        tcol = sb("tcol", [P, NT], F32)
        zz = sb("zz", [P, 4, NT], F32)
        ab = sb("ab", [P, 2, NT], F32)
        ew = sb("ew", [P, 2, NT], F32)
        tt = sb("tt", [P, 10], F32)
        gg = sb("gg", [P, 8], F32)
        den = sb("den", [P, NT], F32)
        rg = sb("rg", [P, NT], F32)
        rden = sb("rden", [P, NT], F32)
        bad = sb("bad", [P, NT + 4], F32)
        flag = sb("flag", [P, 1], I32)
        neg_half = sb("neg_half", [P, 1], F32)
        neg_one = sb("neg_one", [P, 1], F32)
        eps_col = sb("eps_col", [P, 1], F32)
        uf = sb("uf", [P, 2, CT, NF], F32)
        wsq = uf[:, 0, 0, 0:DIN]
        vf = sb("vf", [P, 2, CT, NF], F32)
        tx = sb("tx", [P, 3], F32)

        ps_t = ctx.enter_context(nc.psum_tensor("ps_t", [P, 4, 512], F32))
        ps_a = ctx.enter_context(nc.psum_tensor("ps_a", [P, 4, 512], F32))

        def tbank(i):
            return ps_t[:, i, :].bitcast(BF16)

        adj_loaded = [sem(f"adj_loaded{i}") for i in range(2 * PER)]
        x_loaded = [sem(f"x_loaded{i}") for i in range(NCH // 2)]
        w_loaded = sem("w_loaded")
        constants_ready = sem("constants_ready")
        b_spread = sem("b_spread")
        norms_ready = sem("norms_ready")
        w_turned = sem("w_turned")
        wT_ready = sem("wT_ready")
        wa_done = sem("wa_done")
        wa_ready = sem("wa_ready")
        dve_chain = sem("dve_chain")
        pool_chain = sem("pool_chain")
        bound_ready = sem("bound_ready")
        var_ready = sem("var_ready")
        std_ready = sem("std_ready")
        rstd_ready = sem("rstd_ready")
        normal_dve = sem("normal_dve")
        normal_pool = sem("normal_pool")
        x_turned = sem("x_turned")
        relu_ready = sem("relu_ready")
        h_done = sem("h_done")
        h_ready = sem("h_ready")
        t_row_ready = sem("t_row_ready")
        exponents_ready = sem("exponents_ready")
        weights_ready = sem("weights_ready")
        u_scaled = sem("u_scaled")
        u_high = sem("u_high")
        u_low = sem("u_low")
        v_scaled = sem("v_scaled")
        v_high = sem("v_high")
        v_low = sem("v_low")
        b_loaded = sem("b_loaded")
        shift_ready = sem("shift_ready")
        s_ready = sem("s_ready")
        gates_ready = sem("gates_ready")
        t_ready = sem("t_ready")
        ones_ready = sem("ones_ready")
        t_limits = sem("t_limits")
        neg_s_ready = sem("neg_s_ready")
        factors_ready = sem("factors_ready")
        identb_ready = sem("identb_ready")
        xb_ready = sem("xb_ready")
        sgn_ready = sem("sgn_ready")
        code_ready = sem("code_ready")
        code_turned = sem("code_turned")
        d_ready = sem("d_ready")
        c_ready = sem("c_ready")
        mm_done = sem("mm_done")
        c_scaled = sem("c_scaled")
        sums_ready = sem("sums_ready")
        den_ready = sem("den_ready")
        rden_ready = sem("rden_ready")
        rg_ready = sem("rg_ready")
        pair_summed = sem("pair_summed")
        scaled = sem("scaled")
        rows_ready = sem("rows_ready")
        last_rows = sem("last_rows")
        stored = sem("stored")
        bad_ready = sem("bad_ready")
        flag_ready = sem("flag_ready")
        gen_adj = sem("gen_adj")
        gen_dve = sem("gen_dve")
        gen_scores = sem("gen_scores")
        gen_weights = sem("gen_weights")
        gen_turned = sem("gen_turned")
        gen_copied = sem("gen_copied")
        gen_products = sem("gen_products")
        gen_rows = sem("gen_rows")
        gen_stored = sem("gen_stored")

        adj_t = adj.rearrange("(g p) n -> p g n", p=P)
        x_t = x.rearrange("(g p) d -> p g d", p=P)
        out_t = out.rearrange("(g p) d -> p g d", p=P)

        def chained(eng, s):
            count = [0]

            def step(ins):
                count[0] += 1
                ins.then_inc(s, 1)
                eng.wait_ge(s, count[0])
            return step

        with nc.Block() as block:
            def rounds(eng, body, first=1):
                for it in range(first):
                    body(it)
                with eng.Fori(first, NIT - 1) as it:
                    body(it)
                body(NIT - 1)

            def past(eng, s, it, per, value):
                if isinstance(it, int):
                    if per * it + value > 0:
                        eng.wait_ge(s, per * it + value)
                else:
                    eng.wait_ge(s, it * per + value)

            def last_round(it):
                return isinstance(it, int) and it == NIT - 1

            def hooked(step, before):
                def body(it):
                    for n in range(PER * NB):
                        if isinstance(it, int) and it == 0 and n in before:
                            before[n]()
                        step(it, n)
                return body

            def finish_step(k, stage):
                return NB * (k + 1) - 1 + BEHIND + stage

            def finishes(it, n, stages, finish):
                for k in range(PER):
                    for stage in stages:
                        back, at = divmod(finish_step(k, stage), PER * NB)
                        if at == n and not (isinstance(it, int) and it < back):
                            finish(it - back, k, stage)

            def finishes_after(stages, finish):
                for k in range(PER):
                    for stage in stages:
                        if finish_step(k, stage) >= PER * NB:
                            finish(NIT - 1, k, stage)

            @block.sync
            def _(sp):
                def load_x(c):
                    r = slice(2 * c * CT, 2 * (c + 1) * CT)
                    sp.dma_start(x_sb[:, r, :], x_t[:, r, :]).then_inc(x_loaded[c], 16)

                load_x(0)
                sp.dma_start(Wn[:], W).then_inc(w_loaded, 16)
                for k in range(2):
                    sp.dma_start(a_sb[:, k:k + 1], a_vec[k * P:(k + 1) * P].rearrange("(p a) -> p a", a=1)
                                 ).then_inc(w_loaded, 16)
                sp.dma_start(b_col[:], b_W.rearrange("(p a) -> p a", a=1)).then_inc(w_loaded, 16)
                for c in range(1, NCH // 2):
                    load_x(c)
                sp.dma_start(ba_row[:], b_a.rearrange("(a n) -> a n", a=1).to_broadcast([P, 1])).then_inc(b_loaded, 16)
                sp.dma_start(b_row[:], b_W.rearrange("(a n) -> a n", a=1).to_broadcast([P, DOUT])).then_inc(b_loaded, 16)
                for h in range(2 * PER):
                    sp.dma_start(adj_sb[:, h, :],
                                 adj_t[:, h // 2, (h % 2) * QC:(h % 2 + 1) * QC]).then_inc(adj_loaded[h], 16)

                def load(it):
                    tile = [sp.snap(it * PER + k) if not isinstance(it, int) else it * PER + k for k in range(PER)]
                    for h in range(2 * PER):
                        past(sp, sgn_ready, it, 2 * PER, h + 1 - 2 * PER)
                        sp.dma_start(adj_sb[:, h:h + 1, :],
                                     adj_t[:, bass.ds(tile[h // 2], 1), (h % 2) * QC:(h % 2 + 1) * QC]
                                     ).then_inc(adj_loaded[h], 16)

                def store(it):
                    first = it * PER if isinstance(it, int) else sp.snap(it * PER)
                    if last_round(it):
                        sp.wait_ge(rows_ready, NT - 1)
                        sp.wait_ge(last_rows, 2)
                    else:
                        past(sp, rows_ready, it, PER, PER)
                    sp.dma_start(out_t[:, bass.ds(first, PER), :],
                                 Z[:, bass.ds(first, PER), 0:DOUT]).then_inc(stored, 16)

                load(1)
                with sp.Fori(2, NIT) as it:
                    load(it)
                    store(it - 2)
                store(NIT - 2)
                store(NIT - 1)
                sp.wait_ge(stored, 16 * NIT)

            @block.scalar
            def _(act):
                def signs(it, h):
                    past(act, adj_loaded[h], it, 16, 16)
                    past(act, code_ready, it, PER * NB, 2 * h + 2 - PER * NB)
                    nc.scalar.activation(sgn[:, h // 2, (h % 2) * QC:(h % 2 + 1) * QC], adj_sb[:, h, :], ACT.Sign,
                                         bias=neg_half[:, 0:1]).then_inc(sgn_ready, 1)

                def c_part(it, n):
                    past(act, d_ready, it, PER * NB, n + 1)
                    past(act, mm_done, it, PER * NB, n + 1 - 4)
                    nc.scalar.activation(cT[:, n % 4, :], tbank(n % 4), ACT.Relu,
                                         bias=neg_one[:, 0:1]).then_inc(c_ready, 1)

                def finish(it, k, stage):
                    past(act, mm_done, it, PER * NB, NB * (k + 1))
                    past(act, rows_ready, it, PER, k + 1 - PER)
                    nc.scalar.activation(fin[:, k, 0, :], ps_a[:, 2 * k, 0:2 * NF], ACT.Copy,
                                         scale=ab[:, 0, bass.ds(it * PER + k, 1)]).then_inc(c_scaled, 1)

                def relu_chunk(c):
                    act.wait_ge(x_turned, c + 1)
                    if c >= 2:
                        act.wait_ge(h_done, c - 1)
                    nc.scalar.activation(hT[:, (c % 2) * CT * P:(c % 2 + 1) * CT * P], ps_t[:, c % 2, :],
                                         ACT.Relu).then_inc(relu_ready, 1)

                def take_chunk(c):
                    act.wait_ge(h_done, c + 1)
                    nc.scalar.activation(t_row[:, c * CT * P:(c + 1) * CT * P], ps_t[:, 2 + c % 2, :],
                                         ACT.Identity, bias=cc[:, 1:2]).then_inc(t_row_ready, 1)
                    act.wait_ge(t_ready, c + 1)
                    k = 2 * (c % 2)
                    nc.scalar.activation(
                        H[:, c * CT:(c + 1) * CT, 0:DOUT].rearrange("p (k a) n -> p k a n", k=2),
                        ps_a[:, k:k + 2, 0:2 * (DOUT + 2)].rearrange("p k (a n) -> p k a n", a=2)[:, :, :, 0:DOUT],
                        ACT.Copy).then_inc(h_ready, 1)

                def high(c):
                    act.wait_ge(v_scaled, c + 1)
                    nc.scalar.activation(V[:, c * CT:(c + 1) * CT, 0:NF], vf[:, c % 2], ACT.Copy).then_inc(v_high, 1)

                def std(q):
                    r = slice(2 * CT * q, 2 * CT * (q + 1))
                    act.wait_ge(var_ready, q + 1)
                    nc.scalar.activation(rstd[:, 0, r], mv[:, r, 1], ACT.Sqrt, bias=eps_col[:, 0:1]).then_inc(std_ready, 1)

                def weights(q):
                    r = slice(2 * CT * q, 2 * CT * (q + 1))
                    if q == 0:
                        act.wait_ge(shift_ready, 1)
                    act.wait_ge(t_ready, 2 * q + 2)
                    nc.scalar.activation(ew[:, 0, r], tcol[:, r], ACT.Exp, bias=tt[:, 2:3]).then_inc(weights_ready, 1)
                    nc.scalar.activation(ew[:, 1, r], tcol[:, r], ACT.Exp, bias=tt[:, 3:4],
                                         scale=SLOPE).then_inc(weights_ready, 1)

                def row_factors():
                    act.wait_ge(exponents_ready, 2)
                    nc.scalar.activation(ab[:, 0, :], zz[:, 1, :], ACT.Exp).then_inc(factors_ready, 1)
                    nc.scalar.activation(ab[:, 1, :], zz[:, 3, :], ACT.Exp).then_inc(factors_ready, 1)
                    act.wait_ge(factors_ready, 2)

                act.wait_ge(constants_ready, 1)
                std(0)
                act.wait_ge(norms_ready, 1)
                nc.scalar.activation(gg[:, 1:2], gg[:, 0:1], ACT.Sqrt).then_inc(norms_ready, 1)
                relu_chunk(0)
                act.wait_ge(wa_ready, 3)

                def first_signs(o):
                    signs(0, o)

                after = {
                    0: [(first_signs, 0), (std, 2)],
                    1: [(first_signs, 1)],
                    3: [(high, 0)],
                    4: [(weights, 1), (high, 1)],
                    5: [(weights, 2), (high, 2)],
                    6: [(high, 3)],
                    7: [(weights, 3), (high, 4)],
                }
                std(1)
                for c in range(NCH):
                    if c == 2:
                        std(3)
                    if c + 1 < NCH:
                        relu_chunk(c + 1)
                    if c == 3:
                        weights(0)
                    take_chunk(c)
                    for piece, at in after.get(c, []):
                        piece(at)

                before = {
                    0: lambda: (signs(0, 2), high(5)),
                    1: lambda: (high(6), signs(0, 3), high(7)),
                    5: row_factors,
                }

                def signs_ahead(it, n):
                    o = n // 2 + AHEAD
                    if o < 2 * PER:
                        signs(it, o)
                    elif not last_round(it):
                        signs(it + 1, o - 2 * PER)

                next_signs = [1, 3, 6]

                def step(it, n):
                    start = isinstance(it, int) and it == 0
                    if n % 2 == 0 and not start:
                        signs_ahead(it, n)
                    c_part(it, n)
                    if start and n in next_signs:
                        signs(1, next_signs.index(n))
                    finishes(it, n, [0], finish)

                rounds(act, hooked(step, before), first=2)
                finishes_after([0], finish)

            @block.vector
            def _(dve):
                step_ = chained(dve, dve_chain)

                def codes(it, n):
                    past(dve, sgn_ready, it, 2 * PER, n // 2 + 1)
                    past(dve, code_turned, it, PER * NB, n + 1 - PER * NB)
                    r = slice((n % NB) * BC, (n % NB + 1) * BC)
                    nc.vector.scalar_tensor_tensor(code[:, n // NB, r], t_row[:, r],
                                                   negs[:, bass.ds(it * PER + n // NB, 1)],
                                                   sgn[:, n // NB, r], ALU.is_gt, ALU.add).then_inc(code_ready, 1)

                def d_part(it, n):
                    past(dve, code_turned, it, PER * NB, n + 1)
                    past(dve, mm_done, it, PER * NB, n + 1 - 4)
                    nc.vector.tensor_scalar(dT[:, n % 4, :], tbank(n % 4), 1.0, None,
                                            ALU.is_equal).then_inc(d_ready, 1)

                def finish(it, k, stage):
                    g = bass.ds(it * PER + k, 1)
                    if stage == 1:
                        past(dve, c_scaled, it, PER, k + 1)
                        nc.vector.scalar_tensor_tensor(fin[:, k, 1, :], ps_a[:, 2 * k + 1, 0:2 * NF],
                                                       ab[:, 1, g], fin[:, k, 0, :],
                                                       ALU.mult, ALU.add).then_inc(sums_ready, 1)
                    elif stage == 2:
                        past(dve, sums_ready, it, PER, k + 1)
                        nc.vector.tensor_tensor(den[:, g], fin[:, k, 1, 2 * NF - 1:2 * NF],
                                                fin[:, k, 1, DOUT:NF], ALU.add).then_inc(den_ready, 1)
                    elif stage == 3:
                        past(dve, den_ready, it, PER, k + 1)
                        nc.vector.reciprocal(rden[:, g], den[:, g]).then_inc(rden_ready, 1)
                    else:
                        past(dve, rden_ready, it, PER, k + 1)
                        nc.vector.tensor_scalar(rg[:, g], rden[:, g], gg[:, 3:4], None,
                                                ALU.mult).then_inc(rg_ready, 1)

                def statistics(q):
                    dve.wait_ge(x_loaded[q], 16)
                    for g in range(2 * CT * q, 2 * CT * (q + 1)):
                        last = nc.vector.bn_stats(stats[:, g, :], x_sb[:, g, :])
                    step_(last)
                    for g in range(2 * CT * q, 2 * CT * (q + 1)):
                        last = nc.vector.bn_aggr(mv[:, g, :], stats[:, g, :])
                    last.then_inc(var_ready, 1)

                def inverse(q):
                    r = slice(2 * CT * q, 2 * CT * (q + 1))
                    dve.wait_ge(std_ready, q + 1)
                    nc.vector.reciprocal(rstd[:, 1, r], rstd[:, 0, r]).then_inc(rstd_ready, 1)
                    dve.wait_ge(rstd_ready, q + 1)

                def normalise(c):
                    for g in range(c * CT, (c + 1) * CT):
                        last = nc.vector.tensor_scalar(Z[:, g, 0:DIN], x_sb[:, g, :], mv[:, g, 0:1],
                                                       rstd[:, 1, g:g + 1], ALU.subtract, ALU.mult)
                    last.then_inc(normal_dve, 1)

                def s_and_t(c):
                    k = 2 * (c % 2)
                    r = slice(c * CT, (c + 1) * CT)
                    v = ps_a[:, k:k + 2, 0:2 * (DOUT + 2)].rearrange("p k (a n) -> p k a n", a=2)
                    dve.wait_ge(h_done, c + 1)
                    nc.vector.tensor_scalar(scol[:, r].rearrange("p (k a) -> p k a", k=2), v[:, :, :, DOUT],
                                            cc[:, 0:1], None, ALU.add).then_inc(s_ready, 1)
                    nc.vector.tensor_scalar(tcol[:, r].rearrange("p (k a) -> p k a", k=2), v[:, :, :, DOUT + 1],
                                            cc[:, 1:2], None, ALU.add).then_inc(t_ready, 1)
                    dve.wait_ge(s_ready, c + 1)
                    nc.vector.tensor_scalar(negs[:, r], scol[:, r], -1.0, None, ALU.mult).then_inc(neg_s_ready, 1)

                def split_u(q):
                    pair = [(c, uf[:, c % 2], slice(c * CT, (c + 1) * CT)) for c in (2 * q, 2 * q + 1)]
                    dve.wait_ge(weights_ready, 2 * q + 2)
                    for c, f, r in pair:
                        dve.wait_ge(h_ready, c + 1)
                        if q >= 1:
                            dve.wait_ge(u_low, c - 1)
                        nc.vector.tensor_tensor(f, H[:, r, :],
                                                ew[:, 0, r].to_broadcast([P, CT, NF]), ALU.mult).then_inc(u_scaled, 1)
                    for c, f, r in pair:
                        dve.wait_ge(u_scaled, c + 1)
                        nc.vector.tensor_copy(U[:, r, 0:NF], f).then_inc(u_high, 1)
                    for c, f, r in pair:
                        dve.wait_ge(u_high, c + 1)
                        nc.vector.tensor_tensor(U[:, r, NF:2 * NF], f, U[:, r, 0:NF], ALU.subtract).then_inc(u_low, 1)

                statistics(0)
                dve.wait_ge(w_loaded, 64)
                step_(nc.vector.tensor_tensor(wsq, Wn[:], Wn[:], ALU.mult))
                nc.vector.tensor_reduce(gg[:, 0:1], wsq, AX_X, ALU.add).then_inc(norms_ready, 1)
                dve.wait_ge(constants_ready, 1)
                nc.vector.tensor_scalar(b_mat[:], ones[:], b_col[:, 0:1], None, ALU.mult).then_inc(b_spread, 1)
                nc.vector.tensor_scalar(H[:, :, DOUT], ones[:, 0:NT], 1.0, None, ALU.mult).then_inc(ones_ready, 1)
                dve.wait_ge(norms_ready, 2)
                nc.vector.tensor_scalar(gg[:, 2:3], gg[:, 1:2], 1.01 * float(DIN) ** 0.5, 1e-30,
                                        ALU.mult, ALU.max).then_inc(bound_ready, 1)
                inverse(0)
                normalise(0)
                dve.wait_ge(bound_ready, 2)
                step_(nc.vector.reciprocal(gg[:, 6:7], gg[:, 3:4]))
                dve.wait_ge(w_turned, 1)
                nc.vector.tensor_scalar(WT[:, 0:DOUT], ps_a[:, 0, 0:DOUT], gg[:, 6:7], None, ALU.mult).then_inc(wT_ready, 1)
                dve.wait_ge(wa_done, 1)
                nc.vector.tensor_copy(WT[:, DOUT:DOUT + 2], ps_a[:, 1, 0:2]).then_inc(wa_ready, 1)
                nc.vector.tensor_scalar(wa2[:], ones[:], ps_a[:, 1, 1:2], None, ALU.mult).then_inc(wa_ready, 1)
                step_(nc.vector.tensor_copy(cc[:], ps_a[:, 2, 0:2]))
                dve.wait_ge(b_loaded, 32)
                nc.vector.tensor_tensor(cc[:, 0:1], cc[:, 0:1], ba_row[:], ALU.add).then_inc(wa_ready, 1)
                dve.wait_ge(wa_ready, 3)

                def scale_point():
                    dve.wait_ge(t_limits, 2)
                    nc.vector.tensor_scalar(tt[:, 2:3], tx[:, 0:1], -1.0, SHIFT, ALU.mult, ALU.add)
                    nc.vector.tensor_scalar(tt[:, 3:4], tx[:, 0:1], -SLOPE, SHIFT, ALU.mult, ALU.add).then_inc(shift_ready, 1)

                def batch_codes(n):
                    dve.wait_ge(neg_s_ready, 1)
                    dve.wait_ge(t_row_ready, 2 * n + 2)
                    codes(0, n)

                def first_maximum():
                    dve.wait_ge(t_ready, 1)
                    nc.vector.tensor_reduce(tt[:, 0:1], tcol[:, 0:CT], AX_X, ALU.max).then_inc(t_limits, 1)

                def rest(q):
                    statistics(q)
                    inverse(q)

                rest(1)
                normalise(2)
                s_and_t(0)
                first_maximum()
                rest(2)
                s_and_t(1)
                scale_point()
                statistics(3)
                s_and_t(2)
                inverse(3)
                normalise(6)
                s_and_t(3)
                split_u(0)
                s_and_t(4)
                batch_codes(0)
                s_and_t(5)
                split_u(1)
                s_and_t(6)
                batch_codes(1)
                s_and_t(7)
                split_u(2)
                dve.wait_ge(t_ready, NCH)
                nc.vector.tensor_reduce(tt[:, 4:5], tcol[:], AX_X, ALU.max)
                nc.vector.tensor_reduce(tt[:, 5:6], tcol[:], AX_X, ALU.min, negate=True).then_inc(t_limits, 1)
                dve.wait_ge(neg_s_ready, NCH)
                dve.wait_ge(t_row_ready, NCH)

                def row_exponents():
                    dve.wait_ge(t_limits, 4)
                    step_(nc.vector.tensor_tensor(tt[:, 6:7], tx[:, 1:2], tx[:, 0:1], ALU.subtract))
                    nc.vector.tensor_scalar(tt[:, 7:8], tt[:, 6:7], SLOPE, None, ALU.mult)
                    nc.vector.tensor_tensor(tt[:, 8:9], tx[:, 1:2], tx[:, 2:3], ALU.add)
                    nc.vector.tensor_scalar(zz[:, 0, :], scol[:], tx[:, 1:2], 1.0 - SLOPE, ALU.add, ALU.mult)
                    step_(nc.vector.tensor_scalar(zz[:, 2, :], scol[:], tx[:, 1:2], SLOPE - 1.0, ALU.add, ALU.mult))
                    nc.vector.tensor_scalar(zz[:, 1, :], zz[:, 0, :], 0.0, tt[:, 6:7], ALU.min,
                                            ALU.subtract).then_inc(exponents_ready, 1)
                    nc.vector.tensor_scalar(zz[:, 3, :], zz[:, 2, :], 0.0, tt[:, 7:8], ALU.min,
                                            ALU.subtract).then_inc(exponents_ready, 1)
                    nc.vector.tensor_scalar(bad[:, NT:NT + 1], tt[:, 8:9], SPREAD_MAX, -1.0, ALU.is_le, ALU.mult)
                    nc.vector.tensor_scalar(bad[:, NT + 1:NT + 2], tt[:, 6:7], SHIFT_MAX, -1.0, ALU.is_le,
                                            ALU.mult).then_inc(gates_ready, 1)

                def step(it, n):
                    if n + CODES < PER * NB:
                        codes(it, n + CODES)
                    elif not last_round(it):
                        codes(it + 1, n + CODES - PER * NB)
                    d_part(it, n)
                    finishes(it, n, [1, 2, 3, 4], finish)

                before = {2: lambda: split_u(3), 4: row_exponents}
                rounds(dve, hooked(step, before))
                finishes_after([1, 2, 3, 4], finish)
                last = PER - 1
                dve.wait_ge(scaled, NT - PER)
                dve.wait_ge(xb_ready, NCH // 2)
                dve.wait_ge(sums_ready, NT)
                nc.vector.tensor_tensor(mix[:, last, 0, :], fin[:, last, 1, 0:DOUT],
                                        fin[:, last, 1, NF:2 * NF - 1], ALU.add).then_inc(last_rows, 1)
                dve.wait_ge(last_rows, 1)
                dve.wait_ge(rg_ready, NT)
                nc.vector.scalar_tensor_tensor(Z[:, NT - 1, 0:DOUT], mix[:, last, 0, :], rg[:, NT - 1:NT],
                                               x_sb[:, NT - 1, :], ALU.mult, ALU.add).then_inc(last_rows, 1)
                dve.wait_ge(den_ready, NT)
                dve.wait_ge(gates_ready, 1)
                nc.vector.tensor_scalar(bad[:, 0:NT], den[:], 0.0, -1.0, ALU.is_gt, ALU.mult).then_inc(bad_ready, 1)
                dve.wait_ge(bad_ready, 1)
                nc.vector.tensor_reduce(bad[:, NT + 2:NT + 3], bad[:, 0:NT + 2], AX_X, ALU.max).then_inc(bad_ready, 1)
                dve.wait_ge(bad_ready, 3)
                nc.vector.tensor_scalar(flag[:], bad[:, NT + 3:NT + 4], 1.0, None, ALU.add).then_inc(flag_ready, 1)

            @block.gpsimd
            def _(pool):
                step = chained(pool, pool_chain)
                nc.gpsimd.memset(ones[:], 1.0)
                nc.gpsimd.memset(neg_half[:], -0.5)
                nc.gpsimd.memset(neg_one[:], -1.0)
                nc.gpsimd.memset(eps_col[:], LN_EPS)
                step(nc.gpsimd.memset(ident[:], 0.0))
                nc.gpsimd.affine_select(out=ident[:], in_=ident[:], compare_op=ALU.not_equal, fill=1.0,
                                        base=0, pattern=[[-1, P]], channel_multiplier=1).then_inc(constants_ready, 1)
                pool.wait_ge(constants_ready, 1)
                nc.gpsimd.tensor_copy(identb[:], ident[:]).then_inc(identb_ready, 1)

                def centre(c):
                    r = slice(c * CT, (c + 1) * CT)
                    pool.wait_ge(var_ready, c // 2 + 1)
                    step(nc.gpsimd.tensor_tensor(Z[:, r, 0:DIN], x_sb[:, r, :],
                                                 mv[:, r, 0].to_broadcast([P, CT, DIN]), ALU.subtract))

                def unit(c):
                    r = slice(c * CT, (c + 1) * CT)
                    pool.wait_ge(rstd_ready, c // 2 + 1)
                    nc.gpsimd.tensor_tensor(Z[:, r, 0:DIN], Z[:, r, 0:DIN],
                                            rstd[:, 1, r].to_broadcast([P, CT, DIN]), ALU.mult).then_inc(normal_pool, 1)

                centre(1)
                pool.wait_ge(bound_ready, 1)
                nc.gpsimd.partition_all_reduce(gg[:, 3:4], gg[:, 2:3], P, RMAX).then_inc(bound_ready, 1)
                unit(1)
                centre(3)
                unit(3)
                pool.wait_ge(t_limits, 1)
                nc.gpsimd.partition_all_reduce(tx[:, 0:1], tt[:, 0:1], P, RMAX).then_inc(t_limits, 1)

                def scale_v(c):
                    r = slice(c * CT, (c + 1) * CT)
                    pool.wait_ge(weights_ready, 2 * (c // 2) + 2)
                    pool.wait_ge(h_ready, c + 1)
                    if c >= 2:
                        pool.wait_ge(v_low, c - 1)
                    nc.gpsimd.tensor_tensor(vf[:, c % 2], H[:, r, :],
                                            ew[:, 1, r].to_broadcast([P, CT, NF]), ALU.mult).then_inc(v_scaled, 1)

                def low_v(c):
                    r = slice(c * CT, (c + 1) * CT)
                    pool.wait_ge(v_high, c + 1)
                    nc.gpsimd.tensor_tensor(V[:, r, NF:2 * NF], vf[:, c % 2], V[:, r, 0:NF],
                                            ALU.subtract).then_inc(v_low, 1)

                for c in BY_POOL[2:]:
                    centre(c)
                    unit(c)
                pool.wait_ge(ones_ready, 1)
                scale_v(0)
                for c in range(NCH):
                    if c + 1 < NCH:
                        scale_v(c + 1)
                    low_v(c)
                pool.wait_ge(t_limits, 3)
                nc.gpsimd.partition_all_reduce(tx[:, 1:3], tt[:, 4:6], P, RMAX).then_inc(t_limits, 1)
                pool.wait_ge(normal_dve, len(BY_DVE))
                pool.wait_ge(b_loaded, 32)
                for q in range(NCH // 2):
                    r = slice(2 * CT * q, 2 * CT * (q + 1))
                    nc.gpsimd.tensor_tensor(x_sb[:, r, :], x_sb[:, r, :],
                                            b_row[:].rearrange("p (a n) -> p a n", a=1).to_broadcast([P, 2 * CT, DIN]),
                                            ALU.add).then_inc(xb_ready, 1)
                pool.wait_ge(xb_ready, NCH // 2)

                def rows(it, k):
                    g = bass.ds(it * PER + k, 1)
                    past(pool, sums_ready, it, PER, k + 1)
                    nc.gpsimd.tensor_tensor(mix[:, k, 0, :], fin[:, k, 1, 0:DOUT],
                                            fin[:, k, 1, NF:2 * NF - 1], ALU.add).then_inc(pair_summed, 1)
                    past(pool, pair_summed, it, PER, k + 1)
                    past(pool, rg_ready, it, PER, k + 1)
                    nc.gpsimd.tensor_tensor(mix[:, k, 1, :], mix[:, k, 0, :],
                                            rg[:, g].to_broadcast([P, DOUT]), ALU.mult).then_inc(scaled, 1)
                    past(pool, scaled, it, PER, k + 1)
                    nc.gpsimd.tensor_tensor(Z[:, g, 0:DOUT], mix[:, k, 1:2, :], x_sb[:, g, :],
                                            ALU.add).then_inc(rows_ready, 1)

                with pool.Fori(0, NIT - 1) as it:
                    for k in range(PER):
                        rows(it, k)
                for k in range(PER - 1):
                    rows(NIT - 1, k)
                pool.wait_ge(bad_ready, 2)
                nc.gpsimd.partition_all_reduce(bad[:, NT + 3:NT + 4], bad[:, NT + 2:NT + 3], P,
                                               RMAX).then_inc(bad_ready, 1)

            @block.tensor
            def _(pe):
                def transposes(it, n):
                    past(pe, code_ready, it, PER * NB, n + 1)
                    past(pe, c_ready, it, PER * NB, n + 1 - 4)
                    for j in range(BT):
                        col = (n % NB) * BC + j * P
                        ins = nc.tensor.transpose(tbank(n % 4)[:, j * P:(j + 1) * P],
                                                  code[:, n // NB, col:col + P], identb[:])
                    ins.then_inc(code_turned, 1)

                def products(it, n):
                    k = n // NB
                    past(pe, c_ready, it, PER * NB, n + 1)
                    if isinstance(it, int) and it == 0 and n < NB:
                        pe.wait_ge(u_low, 2 * n + 2)
                        pe.wait_ge(v_low, 2 * n + 2)
                    if n % NB == 0:
                        past(pe, sums_ready, it, PER, k + 1 - PER)
                    for j in range(BT):
                        jt = (n % NB) * BT + j
                        for m, (part, data) in enumerate(((cT, U), (dT, V))):
                            ins = nc.tensor.matmul(ps_a[:, 2 * k + m, 0:2 * NF], part[:, n % 4, j * P:(j + 1) * P],
                                                   data[:, jt, :], start=(jt == 0), stop=(jt == NT - 1))
                    ins.then_inc(mm_done, 1)

                pe.wait_ge(constants_ready, 1)
                pe.wait_ge(w_loaded, 64)
                nc.tensor.transpose(ps_a[:, 0, 0:P], Wn[:], ident[:]).then_inc(w_turned, 1)
                pe.wait_ge(b_spread, 1)
                nc.tensor.matmul(ps_a[:, 1, 0:2], Wn[:], a_sb[:], start=True, stop=True)
                nc.tensor.matmul(ps_a[:, 2, 0:2], b_mat[:], a_sb[:], start=True, stop=True).then_inc(wa_done, 1)

                def turn_chunk(c):
                    if c in BY_DVE:
                        pe.wait_ge(normal_dve, BY_DVE.index(c) + 1)
                    else:
                        pe.wait_ge(normal_pool, BY_POOL.index(c) + 1)
                    if c >= 2:
                        pe.wait_ge(relu_ready, c - 1)
                    for j in range(CT):
                        last = nc.tensor.transpose(ps_t[:, c % 2, j * P:(j + 1) * P],
                                                   Z[:, c * CT + j, 0:DIN], ident[:])
                    last.then_inc(x_turned, 1)

                turn_chunk(0)
                pe.wait_ge(wa_ready, 3)
                pe.wait_ge(wT_ready, 1)
                for c in range(NCH):
                    if c + 1 < NCH:
                        turn_chunk(c + 1)
                    pe.wait_ge(relu_ready, c + 1)
                    if c >= 2:
                        pe.wait_ge(h_ready, c - 1)
                        pe.wait_ge(t_row_ready, c - 1)
                    h = hT[:, (c % 2) * CT * P:(c % 2 + 1) * CT * P]
                    for j in range(CT):
                        at = (j % 2) * (DOUT + 2)
                        nc.tensor.matmul(ps_a[:, 2 * (c % 2) + j // 2, at:at + DOUT + 2],
                                         h[:, j * P:(j + 1) * P], WT[:], start=(j % 2 == 0), stop=(j % 2 == 1),
                                         skip_group_check=True)
                    nc.tensor.matmul(ps_t[:, 2 + c % 2, :], wa2[:], h, start=True, stop=True).then_inc(h_done, 1)
                pe.wait_ge(identb_ready, 1)
                pe.wait_ge(t_row_ready, NCH)
                pe.wait_ge(h_ready, NCH)

                def step(it, n):
                    if n + LEAD < PER * NB:
                        transposes(it, n + LEAD)
                    elif not last_round(it):
                        transposes(it + 1, n + LEAD - PER * NB)
                    products(it, n)

                for n in range(LEAD):
                    transposes(0, n)
                rounds(pe, hooked(step, {}))

        with nc.Block() as block:
            halves = [adj_sb[:, 0:2, :].rearrange("p a n -> p (a n)"),
                      adj_sb[:, 2:4, :].rearrange("p a n -> p (a n)").bitcast(F32),
                      sgn[:, :, :].rearrange("p a n -> p (a n)").bitcast(F32)]
            conn, score, keep = halves
            pT = hT
            acc = ps_a[:, 0, 0:NF]

            def needed(eng):
                return eng.value_load(flag[0:1, 0:1], min_val=0, max_val=1)

            @block.gpsimd
            def _(pool):
                with pool.If(needed(pool) > 0):
                    with pool.Fori(0, NT) as g:
                        pool.dma_start(conn, adj_t[:, bass.ds(g, 1), :]).then_inc(gen_adj, 16)
                        pool.wait_ge(gen_rows, g + 1)
                        pool.dma_start(out_t[:, bass.ds(g, 1), :], Z[:, bass.ds(g, 1), 0:DOUT]).then_inc(gen_stored, 16)
                        pool.wait_ge(gen_stored, g * 16 + 16)

            @block.vector
            def _(dve):
                with dve.If(needed(dve) > 0):
                    with dve.Fori(0, NT) as g:
                        g1 = bass.ds(g, 1)
                        done = [0]

                        def step(ins):
                            done[0] += 1
                            ins.then_inc(gen_dve, 1)
                            dve.wait_ge(gen_dve, g * STEPS + done[0])

                        dve.wait_ge(gen_adj, g * 16 + 16)
                        step(nc.vector.tensor_scalar(score, t_row[:], scol[:, g1], None, ALU.add))
                        step(nc.vector.scalar_tensor_tensor(score, score, SLOPE, score, ALU.mult, ALU.max))
                        step(nc.vector.tensor_scalar(keep, conn, 0.0, None, ALU.is_gt))
                        step(nc.vector.tensor_tensor(score, score, keep, ALU.mult))
                        step(nc.vector.tensor_scalar(keep, keep, -1.0, -NEG_INF, ALU.add, ALU.mult))
                        step(nc.vector.tensor_tensor(score, score, keep, ALU.add))
                        nc.vector.tensor_reduce(tt[:, 9:10], score, AX_X, ALU.max, negate=True).then_inc(gen_scores, 1)
                        dve.wait_ge(gen_products, g * (NT // 4) + NT // 4)
                        step(nc.vector.reciprocal(rden[:, g1], den[:, g1]))
                        step(nc.vector.tensor_scalar(rg[:, g1], rden[:, g1], gg[:, 3:4], None, ALU.mult))
                        nc.vector.scalar_tensor_tensor(Z[:, g1, 0:DOUT], ps_a[:, 0:1, 0:DOUT], rg[:, g1],
                                                       x_sb[:, g1, :], ALU.mult, ALU.add).then_inc(gen_rows, 1)
                        assert done[0] == STEPS

            @block.scalar
            def _(act):
                with act.If(needed(act) > 0):
                    with act.Fori(0, NT) as g:
                        act.wait_ge(gen_scores, g + 1)
                        nc.scalar.activation(keep, score, ACT.Exp, bias=tt[:, 9:10],
                                             accum_out=den[:, bass.ds(g, 1)]).then_inc(gen_weights, 1)
                        for q in range(NT // 4):
                            act.wait_ge(gen_turned, g * (NT // 4) + q + 1)
                            nc.scalar.activation(pT[:, 0:512], ps_t[:, 0, :], ACT.Copy).then_inc(gen_copied, 1)
                            act.wait_ge(gen_products, g * (NT // 4) + q + 1)

            @block.tensor
            def _(pe):
                with pe.If(needed(pe) > 0):
                    with pe.Fori(0, NT) as g:
                        pe.wait_ge(gen_weights, g + 1)
                        for q in range(NT // 4):
                            for j in range(4):
                                ins = nc.tensor.transpose(ps_t[:, 0, j * P:(j + 1) * P],
                                                          keep[:, (4 * q + j) * P:(4 * q + j + 1) * P], ident[:])
                            ins.then_inc(gen_turned, 1)
                            pe.wait_ge(gen_copied, g * (NT // 4) + q + 1)
                            for j in range(4):
                                jt = 4 * q + j
                                ins = nc.tensor.matmul(acc[:, 0:DOUT], pT[:, j * P:(j + 1) * P], H[:, jt, 0:DOUT],
                                                       start=(jt == 0), stop=(jt == NT - 1))
                            ins.then_inc(gen_products, 1)
                        pe.wait_ge(gen_rows, g + 1)


_INS = ["x", "adj", "L0_gnn_W", "L0_gnn_b_W", "L0_gnn_a_vec", "L0_gnn_b_a"]


def kernel(**inputs):
    import numpy as np
    import concourse.bacc as bacc
    from concourse.bass_utils import run_bass_kernel_spmd

    nc = bacc.Bacc("TRN2", target_bir_lowering=False, num_devices=1)
    arrays, args = {}, []
    for name in _INS:
        a = np.ascontiguousarray(inputs[name])
        arrays[f"in_{name}"] = a
        args.append(nc.dram_tensor(f"in_{name}", a.shape, mybir.dt.from_np(a.dtype), kind="ExternalInput").ap())
    out = nc.dram_tensor("out", arrays["in_x"].shape, mybir.dt.float32, kind="ExternalOutput").ap()
    gat_layer_kernel(nc, *args, out)
    r = run_bass_kernel_spmd(nc, [arrays], core_ids=[0])
    return r.results[0]["out"]
```
